# Optimizing a Trainium2 kernel written in Bass

```python
import numpy as np
import jax
import jax.numpy as jnp

def _softmax(x, axis=-1):
    return jax.nn.softmax(x, axis=axis)

def _gelu(x):
    return jax.nn.gelu(x, approximate=True)

def _silu(x):
    return jax.nn.silu(x)

def _sigmoid(x):
    return jax.nn.sigmoid(x)

def _layernorm(x, axis=-1, eps=1e-05):
    m = jnp.mean(x, axis=axis, keepdims=True)
    v = jnp.var(x, axis=axis, keepdims=True)
    return (x - m) / jnp.sqrt(v + eps)

def _scatter_add(tgt, idx, src, axis=0):
    return tgt.at[idx].add(src)

def _segment_sum(src, seg, n):
    return jax.ops.segment_sum(src, seg, n)
kernel_name = 'mk_sandwich_d1_jaxref_r8_db61d0'

def setup_inputs(seed: int=0):
    np.random.seed(seed)
    _w = jnp.asarray

    def _L0_attn_setup():
        import jax, jax.numpy as jnp
        import numpy as np
        L, H = (2, 16)
        B, T, C = (2, 256, 128)
        EPS = 1e-05

        def layernorm(x, g, b):
            mu = jnp.mean(x, axis=-1, keepdims=True)
            var = jnp.mean((x - mu) ** 2, axis=-1, keepdims=True)
            return (x - mu) / jnp.sqrt(var + EPS) * g + b
        key = jax.random.key(seed)
        ks = jax.random.split(key, 8)
        s = 0.02
        return {'x': jax.random.normal(ks[0], (B, T, C), jnp.float32), 'ln1_g': jnp.ones((L, C), jnp.float32), 'ln1_b': jnp.zeros((L, C), jnp.float32), 'wq': jax.random.normal(ks[1], (L, C, C), jnp.float32) * s, 'bq': jnp.zeros((L, C), jnp.float32), 'wk': jax.random.normal(ks[2], (L, C, C), jnp.float32) * s, 'bk': jnp.zeros((L, C), jnp.float32), 'wv': jax.random.normal(ks[3], (L, C, C), jnp.float32) * s, 'bv': jnp.zeros((L, C), jnp.float32), 'wo': jax.random.normal(ks[4], (L, C, C), jnp.float32) * s, 'bo': jnp.zeros((L, C), jnp.float32), 'ln2_g': jnp.ones((L, C), jnp.float32), 'ln2_b': jnp.zeros((L, C), jnp.float32), 'w1': jax.random.normal(ks[5], (L, C, 4 * C), jnp.float32) * s, 'b1': jnp.zeros((L, 4 * C), jnp.float32), 'w2': jax.random.normal(ks[6], (L, 4 * C, C), jnp.float32) * s, 'b2': jnp.zeros((L, C), jnp.float32), 'lnf_g': jnp.ones((C,), jnp.float32), 'lnf_b': jnp.zeros((C,), jnp.float32)}
    _L0_attn_in = _L0_attn_setup()

    def _L0_ffn_setup():
        import math
        import jax, jax.numpy as jnp
        import numpy as np
        CAPACITY_FACTOR = 1.25
        key = jax.random.key(seed)
        ks = jax.random.split(key, 5)
        B, S, H, F, E = (4, 512, 128, 128, 32)
        scale_in = 1.0 / math.sqrt(H)
        scale_mid = 1.0 / math.sqrt(F)
        return {'x': jax.random.normal(ks[0], (B, S, H), dtype=jnp.float32), 'w_router': jax.random.normal(ks[1], (H, E), dtype=jnp.float32) * scale_in, 'w_gate': jax.random.normal(ks[2], (E, H, F), dtype=jnp.float32) * scale_in, 'w_up': jax.random.normal(ks[3], (E, H, F), dtype=jnp.float32) * scale_in, 'w_down': jax.random.normal(ks[4], (E, F, H), dtype=jnp.float32) * scale_mid}
    _L0_ffn_in = _L0_ffn_setup()
    _d = {'L0_attn_x': _L0_attn_in['x'], 'L0_attn_ln1_g': _L0_attn_in['ln1_g'], 'L0_attn_ln1_b': _L0_attn_in['ln1_b'], 'L0_attn_wq': _L0_attn_in['wq'], 'L0_attn_bq': _L0_attn_in['bq'], 'L0_attn_wk': _L0_attn_in['wk'], 'L0_attn_bk': _L0_attn_in['bk'], 'L0_attn_wv': _L0_attn_in['wv'], 'L0_attn_bv': _L0_attn_in['bv'], 'L0_attn_wo': _L0_attn_in['wo'], 'L0_attn_bo': _L0_attn_in['bo'], 'L0_attn_ln2_g': _L0_attn_in['ln2_g'], 'L0_attn_ln2_b': _L0_attn_in['ln2_b'], 'L0_attn_w1': _L0_attn_in['w1'], 'L0_attn_b1': _L0_attn_in['b1'], 'L0_attn_w2': _L0_attn_in['w2'], 'L0_attn_b2': _L0_attn_in['b2'], 'L0_attn_lnf_g': _L0_attn_in['lnf_g'], 'L0_attn_lnf_b': _L0_attn_in['lnf_b'], 'L0_ffn_w_router': _L0_ffn_in['w_router'], 'L0_ffn_w_gate': _L0_ffn_in['w_gate'], 'L0_ffn_w_up': _L0_ffn_in['w_up'], 'L0_ffn_w_down': _L0_ffn_in['w_down']}
    _x0 = _d['L0_attn_x']
    _d['L0_attn_x'] = jax.random.normal(jax.random.fold_in(jax.random.key(seed), 1), (16, 256, 128), dtype=_x0.dtype)
    del _x0
    return _d

def reference(L0_attn_x, L0_attn_ln1_g, L0_attn_ln1_b, L0_attn_wq, L0_attn_bq, L0_attn_wk, L0_attn_bk, L0_attn_wv, L0_attn_bv, L0_attn_wo, L0_attn_bo, L0_attn_ln2_g, L0_attn_ln2_b, L0_attn_w1, L0_attn_b1, L0_attn_w2, L0_attn_b2, L0_attn_lnf_g, L0_attn_lnf_b, L0_ffn_w_router, L0_ffn_w_gate, L0_ffn_w_up, L0_ffn_w_down):

    def _L0_attn_ref(x, ln1_g, ln1_b, wq, bq, wk, bk, wv, bv, wo, bo, ln2_g, ln2_b, w1, b1, w2, b2, lnf_g, lnf_b):
        import jax, jax.numpy as jnp
        import numpy as np
        L, H = (2, 16)
        B, T, C = (2, 256, 128)
        EPS = 1e-05

        def layernorm(x, g, b):
            mu = jnp.mean(x, axis=-1, keepdims=True)
            var = jnp.mean((x - mu) ** 2, axis=-1, keepdims=True)
            return (x - mu) / jnp.sqrt(var + EPS) * g + b
        Bx, Tx, Cx = x.shape
        hd = Cx // H
        scale = 1.0 / np.sqrt(hd).astype(np.float32)
        rows = jnp.arange(Tx)
        allowed = (rows[:, None] % 3 != 0) | (rows[None, :] <= rows[:, None])
        neg_inf = jnp.float32(float('-inf'))
        for i in range(L):
            h = layernorm(x, ln1_g[i], ln1_b[i])
            q = (h @ wq[i] + bq[i]).reshape(Bx, Tx, H, hd).transpose(0, 2, 1, 3)
            k = (h @ wk[i] + bk[i]).reshape(Bx, Tx, H, hd).transpose(0, 2, 1, 3)
            v = (h @ wv[i] + bv[i]).reshape(Bx, Tx, H, hd).transpose(0, 2, 1, 3)
            att = jnp.einsum('bhqd,bhkd->bhqk', q, k) * scale
            att = jnp.where(allowed[None, None], att, neg_inf)
            att = jax.nn.softmax(att, axis=-1)
            y = jnp.einsum('bhqk,bhkd->bhqd', att, v)
            y = y.transpose(0, 2, 1, 3).reshape(Bx, Tx, Cx)
            x = x + y @ wo[i] + bo[i]
            h2 = layernorm(x, ln2_g[i], ln2_b[i])
            x = x + jax.nn.gelu(h2 @ w1[i] + b1[i], approximate=False) @ w2[i] + b2[i]
        return layernorm(x, lnf_g, lnf_b)

    def _L0_ffn_ref(x, w_router, w_gate, w_up, w_down):
        import math
        import jax, jax.numpy as jnp
        import numpy as np
        CAPACITY_FACTOR = 1.25
        B, S, H = x.shape
        E = w_gate.shape[0]
        T = B * S
        C = int(math.ceil(CAPACITY_FACTOR * T / E))
        xt = x.reshape(T, H)
        logits = xt @ w_router
        probs = jax.nn.softmax(logits, axis=-1)
        top1 = jnp.argmax(probs, axis=-1)
        gate = jnp.take_along_axis(probs, top1[:, None], axis=1)[:, 0]
        onehot = jax.nn.one_hot(top1, E, dtype=jnp.int32)
        pos = jnp.cumsum(onehot, axis=0)[jnp.arange(T), top1] - 1
        accepted = pos < C
        slot = jnp.where(accepted, top1 * C + pos, E * C)
        buf = jnp.zeros((E * C + 1, H), dtype=x.dtype).at[slot].set(xt)
        buf = buf[:E * C].reshape(E, C, H)
        g = jnp.einsum('ech,ehf->ecf', buf, w_gate)
        u = jnp.einsum('ech,ehf->ecf', buf, w_up)
        y = jnp.einsum('ecf,efh->ech', jax.nn.silu(g) * u, w_down)
        out_tok = y.reshape(E * C, H)[jnp.clip(slot, 0, E * C - 1)]
        out_tok = jnp.where(accepted[:, None], out_tok * gate[:, None], 0.0)
        return (xt + out_tok).reshape(B, S, H)
    x = L0_attn_x
    x = x + _layernorm(_L0_attn_ref(_layernorm(x, axis=-1), L0_attn_ln1_g, L0_attn_ln1_b, L0_attn_wq, L0_attn_bq, L0_attn_wk, L0_attn_bk, L0_attn_wv, L0_attn_bv, L0_attn_wo, L0_attn_bo, L0_attn_ln2_g, L0_attn_ln2_b, L0_attn_w1, L0_attn_b1, L0_attn_w2, L0_attn_b2, L0_attn_lnf_g, L0_attn_lnf_b), axis=-1)
    x = x + _layernorm(_L0_ffn_ref(_layernorm(x, axis=-1), L0_ffn_w_router, L0_ffn_w_gate, L0_ffn_w_up, L0_ffn_w_down), axis=-1)
    return x

_drawn_inputs = setup_inputs


def setup_inputs(seed=0):
    import zlib

    import numpy as np

    out = dict(_drawn_inputs(seed))
    spreads = {'L0_attn_ln1_g': (1.0, 0.6),
     'L0_attn_ln1_b': (0.0, 0.8),
     'L0_attn_bq': (0.0, 0.8),
     'L0_attn_bk': (0.0, 2.0),
     'L0_attn_bv': (0.0, 0.494),
     'L0_attn_bo': (0.0, 0.1),
     'L0_attn_ln2_g': (1.0, 0.6),
     'L0_attn_ln2_b': (0.0, 2.0),
     'L0_attn_b1': (0.0, 0.439),
     'L0_attn_b2': (0.0, 0.1),
     'L0_attn_lnf_g': (1.0, 0.2),
     'L0_attn_lnf_b': (0.0, 0.1)}
    factors = {'L0_attn_wq': 8.0, 'L0_attn_wk': 8.0, 'L0_attn_wv': 8.0, 'L0_attn_wo': 3.117}
    for name, (base, spread) in spreads.items():
        noise = np.random.default_rng([zlib.crc32(name.encode()), seed]).standard_normal(out[name].shape)
        drawn = base * np.exp(spread * noise) if base else spread * noise
        out[name] = jnp.asarray(drawn.astype(out[name].dtype))
    for name, factor in factors.items():
        out[name] = (out[name] * factor).astype(out[name].dtype)
    return out
```

```python
from contextlib import ExitStack

import numpy as np
import concourse.bass as bass
from concourse import mybir

F32 = mybir.dt.float32
BF16 = mybir.dt.bfloat16
U32 = mybir.dt.uint32
ALU = mybir.AluOpType
ACT = mybir.ActivationFunctionType
AX = mybir.AxisListType

P = 128
NB, T = 16, 256
H, HD = 16, 8
L = 2
FF = 512
NCH = FF // P
E, CAP = 32, 160
NT = NB * T // P
HALF = CAP // 2
EPS = 1e-5
SCALE = float(np.float32(1.0) / np.sqrt(HD).astype(np.float32))
BIG = -1e38

ROW_MASK = 0
N_MASK = 43
ROW_PROD = 64
ROW_ALL = 112
ROW_MAX = 113
ROWS = 116
BLOCKS = [(0, 0), (0, 1), (0, 2), (1, 0), (1, 1), (2, 0)]

DUMP = E * CAP
FIRST_LOOP, LAST_LOOP = 3, 13


def constants():
    q = np.arange(T)
    qrows = np.zeros((P, T), np.float32)
    krows = np.zeros((P, T), np.float32)
    for j in range(N_MASK):
        qrows[ROW_MASK + j, [3 * j, P + 1 + 3 * j]] = 1.0
        krows[ROW_MASK + j] = np.where(q < P, np.where(q > 3 * j, BIG, 0.0), np.where(q > P + 1 + 3 * j, BIG, 0.0))
    qrows[ROW_ALL] = (q % 3 == 0) & (q < P)
    krows[ROW_ALL] = np.where(q >= P, BIG, 0.0)
    krows[ROW_MAX:ROW_MAX + 3] = 1.0
    ident = np.eye(P, dtype=np.float32)
    tri = np.triu(np.ones((P, P), np.float32))
    rev = np.tile(E - np.arange(E, dtype=np.float32), (P, 1))
    dump = DUMP + np.arange(NT, dtype=np.float32)[None, :] * P + np.arange(P, dtype=np.float32)[:, None]
    return {"qrows": qrows, "krows": krows, "ident": ident, "tri": tri, "rev": rev, "dump": dump}


class Item:

    def __init__(self, n, o, b, layer, parity):
        self.n, self.o, self.b, self.l, self.p = n, o, b, layer, parity


def item_at(n):
    if n < 0 or n > 2 * NB + 3 or n in (1, 3, 2 * NB, 2 * NB + 2):
        return None
    o = n - sum(1 for hole in (1, 3, 2 * NB, 2 * NB + 2) if hole < n)
    return Item(n, o, n // 2 if n % 2 == 0 else (n - 5) // 2, n % 2, o % 2)


class Step:

    def __init__(self, s=None, i=None, c=0):
        def at(d):
            if i is None:
                return item_at(s + d)
            k = c + d
            b = i + k // 2 if k % 2 == 0 else i + (k - 5) // 2
            return Item(None, 2 * i + (k - 2), b, k % 2, k % 2)
        self.cur = at(0)
        self.next = at(1)
        self.proj = at(2)
        raw = at(4)
        self.raw = raw if raw is not None and raw.l == 0 else None
        self.post = at(-1)
        self.last = at(-2)
        self.final = self.last if self.last is not None and self.last.l == 1 else None


def build(nc, ins, out):
    ctx = ExitStack()
    with ctx:
        _build(nc, ctx, ins, out)


def _build(nc, ctx, ins, out):
    def sb(name, shape, dt=F32):
        return ctx.enter_context(nc.sbuf_tensor(name, shape, dt))

    def ps(name, shape, dt=F32):
        return ctx.enter_context(nc.psum_tensor(name, shape, dt))

    sems = {}

    def sem(name):
        if name not in sems:
            sems[name] = ctx.enter_context(nc.semaphore(name))
        return sems[name]

    def due(value):
        return not isinstance(value, int) or value > 0

    def hold(eng, value):
        if value is not None and not isinstance(value, int):
            if eng is nc.vector:
                eng.tensor_copy(scratch[:, 0:1], scratch[:, 1:2])
            else:
                eng.tensor_tensor(scratch[:, 2:3], scratch[:, 3:4], scratch[:, 4:5], ALU.add)

    parts_d = [nc.dram_tensor(f"parts_d{p}", (2, 3, HD, H, T), BF16, kind="Internal").ap() for p in range(2)]
    xbuf_d = nc.dram_tensor("xbuf_d", (DUMP + NB * T, P), F32, kind="Internal").ap()
    ybuf_d = nc.dram_tensor("ybuf_d", (DUMP + P, P), F32, kind="Internal").ap()

    XO = sb("x_outer", [P, NT * P])
    XR = sb("x_inner", [P, NT * P])
    qst = [sb(f"q_stack{p}", [P, H, T], BF16) for p in range(2)]
    kst = [sb(f"k_stack{p}", [P, H, T], BF16) for p in range(2)]
    vpad = [sb(f"v_pad{p}", [P, 2, H, 32]) for p in range(2)]
    probs = sb("probs", [P, 8, 2 * T])
    hn = sb("hn", [P, 2, P])
    hT = sb("hT", [P, T])
    qk32 = sb("qk32", [P, 2 * T])
    rest = sb("rest", [P, 2 * T])
    parts = sb("parts", [P, 3, 2 * T], BF16)
    maxes = [sb(f"maxes{p}", [P, H, 2]) for p in range(2)]
    nm_rest = sb("nm_rest", [P, 2, 16])
    nm_parts = sb("nm_parts", [P, 2, 8, 16], BF16)
    nm_rows = sb("nm_rows", [48, 2, P], BF16)
    yraw = sb("yraw", [P, 2 * T])
    rden = sb("rden", [P, 2 * H])
    yn = sb("yn", [P, 2 * H, HD])
    yT = sb("yT", [P, T])
    hn2 = sb("hn2", [P, 2, P])
    h2T = sb("h2T", [P, T])
    gel = sb("gel", [P, NCH, T])
    fin = sb("fin", [P, 2, P])
    bn = {k: sb(f"bn_{k}", [P, 2, 6]) for k in ("raw", "proj", "post", "f1", "f2", "f3")}
    mv = {k: sb(f"mv_{k}", [P, 2, 2]) for k in bn}
    rs = {k: sb(f"rs_{k}", [P, 2, 2]) for k in bn}
    consts = {k: sb(f"c_{k}", [P, v.shape[1]]) for k, v in constants().items()}
    ident = consts["ident"]
    identb = sb("identb", [P, P], BF16)
    trib = sb("trib", [P, P], BF16)
    onesb = sb("onesb", [P, P], BF16)
    eps_mh = sb("eps_mh", [P, 2, 2])
    wq = [sb(f"wq{l}", [P, P]) for l in range(L)]
    wk = [sb(f"wk{l}", [P, P]) for l in range(L)]
    wv = [sb(f"wv{l}", [P, P]) for l in range(L)]
    wo = [sb(f"wo{l}", [P, P]) for l in range(L)]
    w1 = [sb(f"w1{l}", [P, FF]) for l in range(L)]
    w2 = [sb(f"w2{l}", [P, NCH, P]) for l in range(L)]
    cols = [sb(f"cols{l}", [P, 7 + NCH]) for l in range(L)]
    bo_row = [sb(f"bo_row{l}", [P, 2, P]) for l in range(L)]
    b2_row = [sb(f"b2_row{l}", [P, 2, P]) for l in range(L)]
    lnf = sb("lnf", [P, 2, P])
    wr = sb("wr", [P, E])
    zero = sb("zero", [P, 512])
    scratch = sb("scratch", [P, 5])

    wgate = sb("wgate", [P, E, P])
    wup = sb("wup", [P, E, P])
    wdown = sb("wdown", [P, E, P])
    logits = sb("logits", [P, NT * E])
    slot_in = sb("slot_in", [P, NT], U32)
    slot_out = sb("slot_out", [P, NT], U32)
    small = {k: sb(f"r_{k}", [P, NT]) for k in ("top", "rev", "sum", "gate", "place", "taken", "slot", "to")}
    bn_out = sb("bn_out", [P, NT, 6])
    mv_out = sb("mv_out", [P, NT, 2])
    rs_out = sb("rs_out", [P, NT, 2])
    shift = sb("shift", [P, NT])
    diff = probs[:, 4:6, :].rearrange("p a b -> p (a b)")
    expd = probs[:, 6:8, :].rearrange("p a b -> p (a b)")
    yg = probs[:, :, :].rearrange("p a (b c) -> p (a b) c", c=P)
    cand = gel[:, :, :].rearrange("p a b -> p (a b)")
    onehot = parts[:, 0:2, :].rearrange("p a b -> p (a b)")
    xeT = yraw[:, :].rearrange("p (a b) -> p a b", a=2)[:, :, 0:CAP]
    sg = qk32[:, :].rearrange("p (a b) -> p a b", a=2)[:, :, 0:CAP]
    hid = rest[:, :].rearrange("p (a b) -> p a b", a=2)[:, :, 0:CAP]
    yout = vpad[0][0:HALF, :, :, :].rearrange("p t h c -> p (t h c)").rearrange("p (m n c) -> p m n c", m=4, n=2)

    st_ps = [ps(f"st_ps{i}", [P, 2, T]) for i in range(2)]
    sm_ps = [ps(f"sm_ps{i}", [P, 2, T]) for i in range(2)]
    pv_ps = ps("pv_ps", [P, 2 * T])
    mt_ps = ps("mt_ps", [P, 2, 512], BF16)
    ma_ps = ps("ma_ps", [P, 512])
    mb_ps = ps("mb_ps", [P, 512])

    block = ctx.enter_context(nc.Block())

    def x_of(buf, b):
        if isinstance(b, int):
            return buf[:, b * 2 * P:(b + 1) * 2 * P]
        return buf[:, bass.ds(b * (2 * P), 2 * P)]

    def tiles(ap):
        return ap.rearrange("p (t c) -> p t c", t=2)

    def tile_of(buf, b, t):
        if isinstance(b, int):
            return buf[:, (2 * b + t) * P:(2 * b + t + 1) * P]
        return buf[:, bass.ds(b * (2 * P) + t * P, P)]

    def run_steps(eng, step):
        for s in range(-4, 2 * FIRST_LOOP):
            step(Step(s), None)
        with eng.Fori(FIRST_LOOP, LAST_LOOP + 1) as i:
            for c in range(2):
                step(Step(i=i, c=c), (i, c))
        for s in range(2 * LAST_LOOP + 2, 2 * NB + 6):
            step(Step(s), None)

    N_LOADS = 6 + L * (4 + 48 + 6 + NCH + 4) + 3


    def xt_tile(n):
        return XR[:, n * P:(n + 1) * P]

    def expert_rows(q):
        buf = (qst[0], qst[1], kst[0], kst[1])[q]
        return buf[0:HALF, :, :].rearrange("p h t -> p (h t)").bitcast(F32).rearrange("p (n c) -> p n c", c=P)

    def sync_tail(sp):
        sp.wait_ge(sem("scattered"), 16 * NT)
        for q in range(4):
            rows = xbuf_d[q * 8 * CAP:(q + 1) * 8 * CAP, :].rearrange("(n p) c -> p n c", p=HALF)
            sp.dma_start(expert_rows(q), rows).then_inc(sem(f"buf_in{q}"), 16)
        for e in range(E):
            sp.wait_ge(sem("y_out"), e + 1)
            rows = ybuf_d[e * CAP:(e + 1) * CAP, :].rearrange("(n p) c -> p n c", p=HALF)
            sp.dma_start(rows, yout[:, e % 4, :, :]).then_inc(sem(f"y_stored{e % 4}"), 16)
        ov = out.rearrange("b (t p) c -> p (b t) c", p=P)
        for g in range(NT // 4):
            sp.wait_ge(sem("result"), g + 1)
            sp.dma_start(ov[:, 4 * g:4 * g + 4, :], XO[:, g * 4 * P:(g + 1) * 4 * P].rearrange("p (n c) -> p n c", c=P)
                         ).then_inc(sem("stored"), 16)
        sp.wait_ge(sem("stored"), 16 * (NT // 4))

    def pool_tail(pool):
        pool.wait_ge(sem("dram_zero"), 16 * (DUMP // (4 * P) + 1))
        pool.wait_ge(sem("slots"), 1)
        pool.wait_ge(sem("xt"), NB)
        for n in range(NT):
            pool.indirect_dma_start(xbuf_d, bass.IndirectOffsetOnAxis(ap=slot_in[:, n:n + 1], axis=0),
                                    xt_tile(n), None).then_inc(sem("scattered"), 16)
        for m in range(4):
            pool.wait_ge(sem(f"y_stored{m}"), 16 * (E // 4))
        for n in range(NT):
            pool.indirect_dma_start(yg[:, n, :], None, ybuf_d,
                                    bass.IndirectOffsetOnAxis(ap=slot_out[:, n:n + 1], axis=0)).then_inc(sem(f"y_in{n // 4}"), 16)
        for g in range(NT // 4):
            s = slice(4 * g, 4 * g + 4)
            pool.wait_ge(sem("mv_out"), 4 * g + 4)
            pool.tensor_tensor(rs_out[:, s, 0], mv_out[:, s, 1], eps_mh[:, 0:1, 0].to_broadcast([P, 4]), ALU.add).then_inc(sem("ve_out"), 1)
            pool.wait_ge(sem("ve_out"), g + 1)
            pool.tensor_tensor(rs_out[:, s, 1], rs_out[:, s, 0], eps_mh[:, 0:1, 1].to_broadcast([P, 4]), ALU.pow).then_inc(sem("rs_out"), 1)
        for g in range(NT // 4):
            s = slice(g * 4 * P, (g + 1) * 4 * P)
            pool.wait_ge(sem("normed"), g + 1)
            pool.tensor_tensor(XO[:, s], XO[:, s], XR[:, s], ALU.add).then_inc(sem("result"), 1)

    def scalar_tail(act):
        for g in range(NT // 4):
            act.wait_ge(sem("rt_mm"), g + 1)
            if due(g - 3):
                act.wait_ge(sem("lg_mm"), g - 3)
            act.activation(probs[:, g % 4, :], (ma_ps, mb_ps)[g % 2][:, :], ACT.Copy).then_inc(sem("rt_in"), 1)
        act.wait_ge(sem("lg_diff"), 1)
        act.activation(expd[:, :], diff[:, :], ACT.Exp).then_inc(sem("expd"), 1)
        for e in range(E):
            act.wait_ge(sem("et_mm"), e + 1)
            if due(e - 1):
                act.wait_ge(sem("gu_mm"), e - 1)
            act.activation(xeT[:, e % 2, :], st_ps[e % 2][:, 0, 0:CAP], ACT.Copy).then_inc(sem("xeT"), 1)
            act.wait_ge(sem("gu_mm"), e + 1)
            if due(e - 1):
                act.wait_ge(sem("act"), e - 1)
            act.activation(sg[:, e % 2, :], sm_ps[e % 2][:, 0, 0:CAP], ACT.Silu).then_inc(sem("silu"), 1)
        for n in range(NT):
            act.wait_ge(sem("shift"), n // 4 + 1)
            last = act.activation(xt_tile(n), xt_tile(n), ACT.Identity, scale=rs_out[:, n, 1:2], bias=shift[:, n:n + 1])
            if n % 4 == 3:
                last.then_inc(sem("normed"), 1)

    def vector_tail(dve):
        lg = logits[:, :].rearrange("p (n e) -> p n e", e=E)
        df = diff[:, :].rearrange("p (n e) -> p n e", e=E)
        ex = expd[:, :].rearrange("p (n e) -> p n e", e=E)
        cd = cand[:, :].rearrange("p (n e) -> p n e", e=E)
        oh = onehot[:, :].rearrange("p (n e) -> p n e", e=E)

        def wide(ap):
            return ap.rearrange("p (n o) -> p n o", o=1).to_broadcast([P, NT, E])

        n_link = [0]

        def link(ins):
            n_link[0] += 1
            ins.then_inc(sem("route"), 1)
            dve.wait_ge(sem("route"), n_link[0])

        for m in range(2):
            dve.wait_ge(sem("lg_mm"), 4 * m + 4)
            dve.tensor_copy(logits[:, 512 * m:512 * m + 512], st_ps[m][:, :, :].rearrange("p a b -> p (a b)")).then_inc(sem("lg"), 1)
        dve.wait_ge(sem("lg"), 2)
        link(dve.tensor_reduce(small["top"][:, :], lg, AX.X, ALU.max))
        dve.tensor_tensor(df, lg, wide(small["top"][:, :]), ALU.subtract).then_inc(sem("lg_diff"), 1)
        dve.wait_ge(sem("lg_diff"), 1)
        link(dve.scalar_tensor_tensor(out=cd, in0=df, scalar=0.0,
                                      in1=consts["rev"][:, :].rearrange("p (o e) -> p o e", o=1).to_broadcast([P, NT, E]),
                                      op0=ALU.is_ge, op1=ALU.mult))
        link(dve.tensor_reduce(small["rev"][:, :], cd, AX.X, ALU.max))
        dve.tensor_tensor(oh, cd, wide(small["rev"][:, :]), ALU.is_equal).then_inc(sem("onehot"), 1)
        dve.wait_ge(sem("expd"), 1)
        link(dve.tensor_reduce(small["sum"][:, :], ex, AX.X, ALU.add))
        link(dve.reciprocal(small["gate"][:, :], small["sum"][:, :]))
        dve.wait_ge(sem("tot_mm"), 2)
        for m, bank in enumerate((ma_ps, mb_ps)):
            link(dve.tensor_copy(diff[:, 512 * m:512 * m + 512], bank[:, :]))
        a, b, d = diff, expd, 1
        while d < NT:
            link(dve.tensor_tensor(b[:, d * E:], a[:, d * E:], a[:, 0:(NT - d) * E], ALU.add))
            link(dve.tensor_copy(b[:, 0:d * E], a[:, 0:d * E]))
            a, b, d = b, a, 2 * d
        dve.wait_ge(sem("inc_mm"), 2)
        for m, bank in enumerate(sm_ps):
            src = bank[:, :, :].rearrange("p a b -> p (a b)")
            if m == 0:
                link(dve.tensor_copy(logits[:, 0:E], src[:, 0:E]))
                link(dve.tensor_tensor(logits[:, E:512], src[:, E:512], a[:, 0:512 - E], ALU.add))
            else:
                link(dve.tensor_tensor(logits[:, 512:1024], src, a[:, 512 - E:1024 - E], ALU.add))
        link(dve.tensor_tensor(logits[:, :], logits[:, :], onehot[:, :], ALU.mult))
        link(dve.tensor_reduce(small["place"][:, :], lg, AX.X, ALU.add))
        link(dve.tensor_single_scalar(small["taken"][:, :], small["place"][:, :], float(CAP), ALU.is_le))
        link(dve.scalar_tensor_tensor(out=small["slot"][:, :], in0=small["rev"][:, :], scalar=-float(CAP),
                                      in1=small["place"][:, :], op0=ALU.mult, op1=ALU.add))
        link(dve.tensor_scalar(small["slot"][:, :], small["slot"][:, :], float(E * CAP - 1), None, ALU.add))
        link(dve.tensor_tensor(small["to"][:, :], small["slot"][:, :], consts["dump"][:, :], ALU.subtract))
        link(dve.tensor_tensor(small["to"][:, :], small["to"][:, :], small["taken"][:, :], ALU.mult))
        link(dve.tensor_tensor(slot_in[:, :], small["to"][:, :], consts["dump"][:, :], ALU.add))
        link(dve.tensor_scalar(small["slot"][:, :], small["slot"][:, :], -float(DUMP), None, ALU.add))
        link(dve.tensor_tensor(small["slot"][:, :], small["slot"][:, :], small["taken"][:, :], ALU.mult))
        dve.tensor_scalar(slot_out[:, :], small["slot"][:, :], float(DUMP), None, ALU.add).then_inc(sem("slots"), 1)
        for e in range(E):
            dve.wait_ge(sem("silu"), e + 1)
            if due(e - 1):
                dve.wait_ge(sem("ye_mm"), e - 1)
            dve.tensor_tensor(hid[:, e % 2, :], sm_ps[e % 2][:, 1, 0:CAP], sg[:, e % 2, :], ALU.mult).then_inc(sem("act"), 1)
            if e >= 1:
                take_y(dve, e - 1)
        take_y(dve, E - 1)
        for g in range(NT // 4):
            for n in range(4 * g, 4 * g + 4):
                dve.wait_ge(sem(f"y_in{g}"), 64)
                dve.scalar_tensor_tensor(out=xt_tile(n), in0=yg[:, n, :], scalar=small["gate"][:, n:n + 1], in1=xt_tile(n),
                                         op0=ALU.mult, op1=ALU.add).then_inc(sem("z"), 1)
            for n in range(4 * g, 4 * g + 4):
                dve.wait_ge(sem("z"), n + 1)
                dve.bn_stats(bn_out[:, n, :], xt_tile(n)).then_inc(sem("bn_out"), 1)
            for n in range(4 * g, 4 * g + 4):
                dve.wait_ge(sem("bn_out"), n + 1)
                dve.bn_aggr(mv_out[:, n, :], bn_out[:, n, :]).then_inc(sem("mv_out"), 1)
            if g >= 1:
                minus_mean(dve, g - 1)
        minus_mean(dve, NT // 4 - 1)

    def minus_mean(dve, g):
        s = slice(4 * g, 4 * g + 4)
        dve.wait_ge(sem("rs_out"), g + 1)
        dve.scalar_tensor_tensor(out=shift[:, s], in0=mv_out[:, s, 0], scalar=-1.0, in1=rs_out[:, s, 1],
                                 op0=ALU.mult, op1=ALU.mult).then_inc(sem("shift"), 1)

    def take_y(dve, e):
        dve.wait_ge(sem("ye_mm"), e + 1)
        if due(e // 4):
            dve.wait_ge(sem(f"y_stored{e % 4}"), 16 * (e // 4))
        dve.tensor_copy(yout[:, e % 4, :, :], (ma_ps, mb_ps)[e % 2][0:HALF, 0:2 * P].rearrange("p (n c) -> p n c", n=2)
                        ).then_inc(sem("y_out"), 1)

    def tensor_tail(pe):
        pe.wait_ge(sem("xt"), NB)
        pe.wait_ge(sem("exp"), 16 * 2 * NB)
        pe.wait_ge(sem("maxed"), 16 * 2 * NB)
        pe.wait_ge(sem("ffn_out"), 2 * NB)

        def route(g):
            pe.wait_ge(sem("rt_in"), g + 1)
            for n in range(4 * g, 4 * g + 4):
                m = n % 16
                last = pe.matmul(st_ps[n // 16][:, m // 8, (m % 8) * E:(m % 8 + 1) * E], probs[:, g % 4, (n % 4) * P:(n % 4 + 1) * P],
                                 wr[:, :], start=True, stop=True)
            last.then_inc(sem("lg_mm"), 1)

        for g in range(NT // 4):
            if due(g - 1):
                pe.wait_ge(sem("rt_in"), g - 1)
            if g == 0:
                pe.wait_ge(sem("gelu"), 4 * 2 * NB)
            for n in range(4):
                last = pe.transpose((ma_ps, mb_ps)[g % 2][:, n * P:(n + 1) * P], xt_tile(4 * g + n), ident[:, :])
            last.then_inc(sem("rt_mm"), 1)
            if g >= 1:
                route(g - 1)
        route(NT // 4 - 1)
        pe.wait_ge(sem("onehot"), 1)
        pe.wait_ge(sem("rt_in"), NT // 4)
        for m in range(2):
            pe.matmul(sm_ps[m][:, :, :].rearrange("p a b -> p (a b)"), trib[:, :], onehot[:, 512 * m:512 * m + 512],
                      start=True, stop=True).then_inc(sem("inc_mm"), 1)
        for m, bank in enumerate((ma_ps, mb_ps)):
            pe.matmul(bank[:, :], onesb[:, :], onehot[:, 512 * m:512 * m + 512], start=True, stop=True).then_inc(sem("tot_mm"), 1)
        pe.wait_ge(sem("experts_in"), 48)
        pe.wait_ge(sem("slots"), 1)

        def turn(e):
            if e % 8 == 0:
                pe.wait_ge(sem(f"buf_in{e // 8}"), 16)
            if due(e - 1):
                pe.wait_ge(sem("xeT"), e - 1)
            for a in range(2):
                last = pe.transpose(st_ps[e % 2][:, 0, a * HALF:(a + 1) * HALF], expert_rows(e // 8)[:, 2 * (e % 8) + a, :],
                                    ident[0:HALF, 0:HALF])
            last.then_inc(sem("et_mm"), 1)

        def down(e):
            pe.wait_ge(sem("act"), e + 1)
            if due(e - 1):
                pe.wait_ge(sem("y_out"), e - 1)
            for a in range(2):
                last = pe.matmul((ma_ps, mb_ps)[e % 2][0:HALF, a * P:(a + 1) * P], hid[:, e % 2, a * HALF:(a + 1) * HALF],
                                 wdown[:, e, :], start=True, stop=True)
            last.then_inc(sem("ye_mm"), 1)

        turn(0)
        for e in range(E):
            if e + 1 < E:
                turn(e + 1)
            pe.wait_ge(sem("xeT"), e + 1)
            if due(e - 1):
                pe.wait_ge(sem("act"), e - 1)
            for k, w in enumerate((wgate, wup)):
                last = pe.matmul(sm_ps[e % 2][:, k, 0:CAP], w[:, e, :], xeT[:, e % 2, :], start=True, stop=True)
            last.then_inc(sem("gu_mm"), 1)
            if e >= 1:
                down(e - 1)
        down(E - 1)

    @block.sync
    def _(sp):
        xv = ins["L0_attn_x"].rearrange("b (t p) c -> p (b t) c", p=P)
        xo = XO[:, :].rearrange("p (n c) -> p n c", c=P)
        sp.dma_start(xo[:, 0:2, :], xv[:, 0:2, :]).then_inc(sem("x_first"), 16)
        loads = []
        for k in consts:
            loads.append((consts[k][:, :], ins["const_" + k]))
        for l in range(L):
            col = lambda name: ins["L0_attn_" + name][l].rearrange("(p o) -> p o", o=1)
            row = lambda name: ins["L0_attn_" + name][l:l + 1, :].to_broadcast([P, P])
            loads += [(wq[l][:, :], ins["L0_attn_wq"][l]), (wk[l][:, :], ins["L0_attn_wk"][l]),
                      (w1[l][:, :], ins["L0_attn_w1"][l]),
                      (w2[l][:, :, :], ins["L0_attn_w2"][l].rearrange("(k p) n -> p k n", p=P))]
            for s in range(2):
                for u in range(2):
                    for g in range(4):
                        a = 64 * s + 16 * g + 8 * u
                        c = 64 * s + 32 * u + 8 * g
                        loads.append((wv[l][:, a:a + HD], ins["L0_attn_wv"][l][:, c:c + HD]))
                        loads.append((wo[l][a:a + HD, :], ins["L0_attn_wo"][l][c:c + HD, :]))
                        loads.append((cols[l][a:a + HD, 6:7], col("bv")[c:c + HD, :]))
            for n, name in enumerate(("ln1_g", "ln1_b", "bq", "bk", "ln2_g", "ln2_b")):
                loads.append((cols[l][:, n:n + 1], col(name)))
            for c in range(NCH):
                loads.append((cols[l][:, 7 + c:8 + c], ins["L0_attn_b1"][l, c * P:(c + 1) * P].rearrange("(p o) -> p o", o=1)))
            for t in range(2):
                loads.append((bo_row[l][:, t, :], row("bo")))
                loads.append((b2_row[l][:, t, :], row("b2")))
        loads.append((lnf[:, 0, :], ins["L0_attn_lnf_g"].rearrange("(o c) -> o c", o=1).to_broadcast([P, P])))
        loads.append((lnf[:, 1, :], ins["L0_attn_lnf_b"].rearrange("(o c) -> o c", o=1).to_broadcast([P, P])))
        loads.append((wr[:, :], ins["L0_ffn_w_router"]))
        for dst, src in loads:
            sp.dma_start(dst, src).then_inc(sem("setup_in"), 16)
        assert len(loads) == N_LOADS, len(loads)
        sp.dma_start(xo[:, 2:, :], xv[:, 2:, :]).then_inc(sem("x_rest"), 16)
        for w, name in ((wgate, "gate"), (wup, "up"), (wdown, "down")):
            sp.dma_start(w[:, :, :], ins["L0_ffn_w_" + name].rearrange("e h f -> h e f")).then_inc(sem("experts_in"), 16)
        sp.wait_ge(sem("zeroed"), 1)
        for n in range(DUMP // (P * 4)):
            sp.dma_start(xbuf_d[n * 4 * P:(n + 1) * 4 * P, :].rearrange("(p r) c -> p (r c)", p=P),
                         zero[:, :]).then_inc(sem("dram_zero"), 16)
        sp.dma_start(ybuf_d[DUMP:DUMP + P, :], zero[:, 0:P]).then_inc(sem("dram_zero"), 16)

        def read_stack(item, g):
            hs = slice(8 * g, 8 * g + 8)
            d = parts_d[item.p]
            if due(16 * item.o - 32 + 8 * g + 8):
                sp.wait_ge(sem("st_mm"), 16 * item.o - 32 + 8 * g + 8)
            sp.wait_ge(sem("stack_const"), 1)
            sp.wait_ge(sem("parts_out"), 96 * item.o + 96)
            for n, (a, _) in enumerate(BLOCKS):
                sp.dma_start(qst[item.p][ROW_PROD + 8 * n:ROW_PROD + 8 * n + 8, hs, :],
                             d[0, a][:, hs, :]).then_inc(sem(f"stack_in{g}"), 16)
            for n, m in ((0, 3), (3, 2), (5, 1)):
                sp.dma_start(kst[item.p][ROW_PROD + 8 * n:ROW_PROD + 8 * (n + m), hs, :],
                             d[1, 0:m].rearrange("a d h t -> (a d) h t")[:, hs, :]).then_inc(sem(f"stack_in{g}"), 16)

        def max_rows(item, g):
            sp.wait_ge(sem("nm_rows"), 2 * item.o + g + 1)
            sp.dma_start(qst[item.p][ROW_MAX:ROW_MAX + 3, 8 * g:8 * g + 8, :],
                         nm_rows[:, g, :]).then_inc(sem(f"max_in{g}"), 16)

        def step(w, _):
            if w.next is not None:
                read_stack(w.next, 1)
            if w.cur is not None:
                max_rows(w.cur, 1)
            if w.proj is not None:
                c = w.proj
                if isinstance(c.o, int):
                    if due(144 * (c.o - 1)):
                        sp.wait_ge(sem("stack_in1"), 144 * (c.o - 1))
                sp.wait_ge(sem("parts"), c.o + 1)
                for a in range(3):
                    for side in range(2):
                        sp.dma_start(parts_d[c.p][side, a].rearrange("d h t -> h d t"),
                                     parts[:, a, side * T:(side + 1) * T]).then_inc(sem("parts_out"), 16)
            if w.next is not None:
                max_rows(w.next, 0)
            if w.proj is not None:
                read_stack(w.proj, 0)

        run_steps(sp, step)
        sync_tail(sp)

    @block.gpsimd
    def _(pool):
        pool.memset(zero[:, :], 0.0).then_inc(sem("zeroed"), 1)
        pool.memset(eps_mh[:, :, 0:1], EPS).then_inc(sem("eps"), 1)
        pool.memset(eps_mh[:, :, 1:2], -0.5).then_inc(sem("eps"), 1)
        for p in range(2):
            pool.memset(vpad[p][:, :, :, :], 0.0).then_inc(sem("v_zero"), 1)
        pool.wait_ge(sem("v_zero"), 2)
        for p in range(2):
            for u in range(2):
                pool.memset(vpad[p][:, :, :, :].rearrange("p t (s u) c -> p (t s) u c", u=2)[:, :, u, 16 + u:17 + u],
                            1.0).then_inc(sem("v_ones"), 1)
        pool.wait_ge(sem("eps"), 2)
        pool.wait_ge(sem("scratch"), 1)

        def rstd(key, o, count):
            pool.wait_ge(sem(f"mv_{key}"), count)
            pool.tensor_tensor(rs[key][:, :, 0:1], mv[key][:, :, 1:2], eps_mh[:, :, 0:1], ALU.add).then_inc(sem(f"ve_{key}"), 1)
            pool.wait_ge(sem(f"ve_{key}"), o + 1)
            pool.tensor_tensor(rs[key][:, :, 1:2], rs[key][:, :, 0:1], eps_mh[:, :, 1:2], ALU.pow).then_inc(sem(f"rs_{key}"), 1)

        def normalize(key, o, count, dst, src, done):
            rstd(key, o, count)
            pool.tensor_tensor(dst, src, mv[key][:, :, 0:1].to_broadcast([P, 2, P]), ALU.subtract).then_inc(sem(f"sub_{key}"), 1)
            pool.wait_ge(sem(f"sub_{key}"), o + 1)
            pool.wait_ge(sem(f"rs_{key}"), o + 1)
            hold(pool, o)
            pool.tensor_tensor(dst, dst, rs[key][:, :, 1:2].to_broadcast([P, 2, P]), ALU.mult).then_inc(sem(done), 1)

        def step(w, _):
            if w.proj is not None:
                o = w.proj.o
                if due(o):
                    pool.wait_ge(sem("hn_mm"), o)
                normalize("proj", o, 2 * o + 2, hn[:, :, :], tiles(x_of(XR, w.proj.b)), "hn")
            if w.post is not None:
                a = w.post
                pool.wait_ge(sem("setup_bo"), L)
                pool.tensor_tensor(tiles(x_of(XR, a.b)), tiles(x_of(XR, a.b)), bo_row[a.l][:, :, :], ALU.add).then_inc(sem("bo_add"), 1)
            if w.final is not None:
                f = w.final.b
                normalize("f1", f, 2 * f + 2, fin[:, :, :], tiles(x_of(XR, f)), "f1_norm")
                pool.wait_ge(sem("f1_norm"), f + 1)
                pool.tensor_tensor(fin[:, :, :], fin[:, :, :], lnf[:, 0:1, :].to_broadcast([P, 2, P]), ALU.mult).then_inc(sem("f1_g"), 1)
                pool.wait_ge(sem("f1_g"), f + 1)
                pool.tensor_tensor(fin[:, :, :], fin[:, :, :], lnf[:, 1:2, :].to_broadcast([P, 2, P]), ALU.add).then_inc(sem("f1_b"), 1)
            if w.proj is not None:
                o = w.proj.o
                pool.wait_ge(sem("qk32"), o + 1)
                if due(o):
                    pool.wait_ge(sem("part1"), o)
                pool.tensor_tensor(rest[:, :], qk32[:, :], parts[:, 0, :], ALU.subtract).then_inc(sem("rest"), 1)
                pool.wait_ge(sem("part1"), o + 1)
                pool.tensor_tensor(parts[:, 2, :], rest[:, :], parts[:, 1, :], ALU.subtract).then_inc(sem("parts"), 1)
            if w.final is not None:
                f = w.final.b
                normalize("f2", f, 2 * f + 2, fin[:, :, :], fin[:, :, :], "f2_norm")
                pool.wait_ge(sem("f2_norm"), f + 1)
                hold(pool, f)
                pool.tensor_tensor(tiles(x_of(XO, f)), tiles(x_of(XO, f)), fin[:, :, :], ALU.add).then_inc(sem("x_attn"), 1)
            if w.post is not None:
                a = w.post
                if due(a.o):
                    pool.wait_ge(sem("hn2_mm"), a.o)
                normalize("post", a.o, 2 * a.o + 2, hn2[:, :, :], tiles(x_of(XR, a.b)), "hn2")
                pool.tensor_tensor(tiles(x_of(XR, a.b)), tiles(x_of(XR, a.b)), b2_row[a.l][:, :, :], ALU.add).then_inc(sem("b2_add"), 1)
            if w.final is not None:
                f = w.final.b
                normalize("f3", f, 2 * f + 2, tiles(x_of(XR, f)), tiles(x_of(XO, f)), "xt")
            if w.raw is not None:
                r = w.raw.b
                normalize("raw", r, 2 * r + 2, tiles(x_of(XR, r)), tiles(x_of(XO, r)), "x_inner")

        run_steps(pool, step)
        pool_tail(pool)

    @block.vector
    def _(dve):
        dve.wait_ge(sem("setup_in"), 16 * N_LOADS)
        dve.tensor_copy(identb[:, :], ident[:, :]).then_inc(sem("dve_const"), 1)
        dve.tensor_copy(trib[:, :], consts["tri"][:, :]).then_inc(sem("dve_const"), 1)
        dve.memset(onesb[:, :], 1.0).then_inc(sem("dve_const"), 1)
        dve.memset(scratch[:, :], 0.0).then_inc(sem("scratch"), 1)
        dve.memset(nm_parts[:, :, :, :], 0.0).then_inc(sem("scratch"), 1)
        dve.wait_ge(sem("scratch"), 2)
        for l in range(L):
            dve.tensor_copy(yraw[:, l * P:(l + 1) * P], cols[l][:, 6:7].to_broadcast([P, P])).then_inc(sem("bv_wide"), 1)
        for p in range(2):
            for buf, key in ((qst, "qrows"), (kst, "krows")):
                for h in range(0, H, 4):
                    last = dve.tensor_copy(buf[p][0:ROWS, h:h + 4, :],
                                           consts[key][0:ROWS, :].rearrange("p (o t) -> p o t", o=1).to_broadcast([ROWS, 4, T]))
        last.then_inc(sem("stack_const"), 1)
        for l in range(L):
            dve.wait_ge(sem("bo_mm"), L)
            dve.tensor_tensor(bo_row[l][:, :, :], bo_row[l][:, :, :], ma_ps[:, l * P:(l + 1) * P].rearrange(
                "p (o c) -> p o c", o=1).to_broadcast([P, 2, P]), ALU.add).then_inc(sem("setup_bo"), 1)

        def stats(key, buf, b):
            hold(dve, b)
            for t in range(2):
                src = buf[:, t, :] if b is None else tile_of(buf, b, t)
                dve.bn_stats(bn[key][:, t, :], src).then_inc(sem(f"bn_{key}"), 1)

        def aggregate(key, o):
            dve.wait_ge(sem(f"bn_{key}"), 2 * o + 2)
            hold(dve, o)
            for t in range(2):
                dve.bn_aggr(mv[key][:, t, :], bn[key][:, t, :]).then_inc(sem(f"mv_{key}"), 1)

        def minus_max(item, g):
            c = 2 * item.o + g
            m = maxes[item.p][:, 8 * g:8 * g + 8, :].rearrange("p h t -> p (h t)")
            dve.wait_ge(sem("maxed"), 16 * item.o + 8 * g + 8)
            if due(c - 1):
                dve.wait_ge(sem("nm_mm"), c - 1)
            n = nm_parts[:, g]
            dve.tensor_scalar(n[:, 0, :], m, -1.0, None, ALU.mult).then_inc(sem("nm0"), 1)
            dve.wait_ge(sem("nm0"), c + 1)
            dve.scalar_tensor_tensor(out=nm_rest[:, 0, :], in0=m, scalar=-1.0, in1=n[:, 0, :],
                                     op0=ALU.mult, op1=ALU.subtract).then_inc(sem("nm1"), 1)
            dve.wait_ge(sem("nm1"), c + 1)
            dve.tensor_copy(n[:, 1, :], nm_rest[:, 0, :]).then_inc(sem("nm2"), 1)
            dve.wait_ge(sem("nm2"), c + 1)
            dve.tensor_tensor(n[:, 2, :], nm_rest[:, 0, :], n[:, 1, :], ALU.subtract).then_inc(sem("nm_parts"), 1)

        def minus_max_rows(item, g):
            c = 2 * item.o + g
            dve.wait_ge(sem("nm_mm"), c + 1)
            if due(16 * item.o):
                dve.wait_ge(sem(f"max_in{g}"), 16 * item.o)
            dve.tensor_copy(nm_rows[:, g, :], mt_ps[0:48, g, 0:P]).then_inc(sem("nm_rows"), 1)

        def step(w, _):
            for j in range(H):
                if w.next is not None:
                    o = w.next.o
                    dve.wait_ge(sem("sm_mm"), 16 * o + j + 1)
                    dve.tensor_reduce(maxes[w.next.p][:, j, :], sm_ps[j % 2][:, :, :], AX.X, ALU.max).then_inc(sem("maxed"), 1)
                if j == 0 and w.cur is not None:
                    minus_max(w.cur, 1)
                if j == 0 and w.proj is not None:
                    if w.proj.l == 0:
                        dve.wait_ge(sem("x_inner"), w.proj.b + 1)
                    if due(w.proj.o):
                        dve.wait_ge(sem("sub_proj"), w.proj.o)
                    stats("proj", XR, w.proj.b)
                if j == 1 and w.proj is not None:
                    aggregate("proj", w.proj.o)
                if j == 2 and w.cur is not None:
                    minus_max_rows(w.cur, 1)
                if j == 2 and w.last is not None:
                    e = w.last
                    dve.wait_ge(sem("w2_mm"), e.o + 1)
                    dve.wait_ge(sem("b2_add"), e.o + 1)
                    dve.tensor_tensor(x_of(XR, e.b), ma_ps[:, 0:2 * P], x_of(XR, e.b), ALU.add).then_inc(sem("ffn_out"), 1)
                if j == 4 and w.post is not None:
                    a = w.post
                    dve.wait_ge(sem("yt_mm"), a.o + 1)
                    src = ma_ps[:, :].rearrange("p (n r) -> p n r", r=32)
                    dve.reciprocal(rden[:, :].rearrange("p (n u) -> p n u", u=2), src[:, :, 16:18]).then_inc(sem("rden"), 1)
                    dve.wait_ge(sem("rden"), a.o + 1)
                    if due(a.o):
                        dve.wait_ge(sem("ynt_mm"), a.o)
                    dve.tensor_tensor(yn[:, :, :].rearrange("p (n u) d -> p n u d", u=2),
                                      src[:, :, 0:16].rearrange("p n (u d) -> p n u d", u=2),
                                      rden[:, :].rearrange("p (n u o) -> p n u o", u=2, o=1).to_broadcast([P, H, 2, HD]),
                                      ALU.mult).then_inc(sem("yn"), 1)
                if j == 5 and w.final is not None:
                    f = w.final.b
                    dve.wait_ge(sem("ffn_out"), w.final.o + 1)
                    if due(f):
                        dve.wait_ge(sem("sub_f1"), f)
                    stats("f1", XR, f)
                    aggregate("f1", f)
                if j == 6 and w.proj is not None:
                    dve.wait_ge(sem("rest"), w.proj.o + 1)
                    dve.tensor_copy(parts[:, 1, :], rest[:, :]).then_inc(sem("part1"), 1)
                if j == 8 and w.next is not None:
                    minus_max(w.next, 0)
                if j == 9 and w.post is not None:
                    a = w.post
                    dve.wait_ge(sem("wo_mm"), a.o + 1)
                    dve.wait_ge(sem("bo_add"), a.o + 1)
                    dve.tensor_tensor(x_of(XR, a.b), ma_ps[:, 0:2 * P], x_of(XR, a.b), ALU.add).then_inc(sem("attn_out"), 1)
                    dve.wait_ge(sem("attn_out"), a.o + 1)
                    if due(a.o):
                        dve.wait_ge(sem("sub_post"), a.o)
                    stats("post", XR, a.b)
                if j == 10 and w.post is not None:
                    aggregate("post", w.post.o)
                if j == 10 and w.next is not None:
                    minus_max_rows(w.next, 0)
                if j == 11 and w.final is not None:
                    f = w.final.b
                    dve.wait_ge(sem("f1_b"), f + 1)
                    if due(f):
                        dve.wait_ge(sem("sub_f2"), f)
                    stats("f2", fin, None)
                    aggregate("f2", f)
                if j == 15 and w.final is not None:
                    f = w.final.b
                    dve.wait_ge(sem("x_attn"), f + 1)
                    if due(f):
                        dve.wait_ge(sem("sub_f3"), f)
                    stats("f3", XO, f)
                    aggregate("f3", f)
                if j == 15 and w.raw is not None:
                    r = w.raw.b
                    if isinstance(r, int) and r == 0:
                        dve.wait_ge(sem("x_first"), 16)
                    elif isinstance(r, int) and r == 1:
                        dve.wait_ge(sem("x_rest"), 16)
                    if due(r):
                        dve.wait_ge(sem("sub_raw"), r)
                    stats("raw", XO, r)
                    aggregate("raw", r)

        run_steps(dve, step)
        vector_tail(dve)

    @block.scalar
    def _(act):
        def step(w, _):
            for j in range(H):
                if w.cur is not None:
                    k = w.cur
                    act.wait_ge(sem("st_mm"), 16 * k.o + j + 1)
                    if due(4 * k.o + j // 4 - 1):
                        act.wait_ge(sem("pv_mm"), 4 * k.o + j // 4 - 1)
                    act.activation(probs[:, j % 8, :], st_ps[j % 2][:, :, :].rearrange("p a b -> p (a b)"),
                                   ACT.Exp, scale=SCALE).then_inc(sem("exp"), 1)
                if j == 1 and w.post is not None:
                    a = w.post
                    act.wait_ge(sem("pv_mm"), 4 * a.o + 4)
                    if due(a.o):
                        act.wait_ge(sem("yt_mm"), a.o)
                    act.activation(yraw[:, :], pv_ps[:, :], ACT.Copy).then_inc(sem("yraw"), 1)
                if j == 1 and w.next is not None:
                    c = w.next
                    act.wait_ge(sem("v_mm"), c.o + 1)
                    if due(4 * (c.o - 1)):
                        act.wait_ge(sem("pv_mm"), 4 * (c.o - 1))
                    act.wait_ge(sem("v_ones"), 4)
                    for u in range(2):
                        dst = vpad[c.p][:, :, :, :].rearrange("p t (n u) c -> p t n u c", u=2)[:, :, :, u, 8 * u:8 * u + HD]
                        src = ma_ps[:, 0:2 * P].rearrange("p (t n u d) -> p t n u d", t=2, u=2, d=HD)[:, :, :, u, :]
                        last = act.activation(dst, src, ACT.Copy)
                    last.then_inc(sem("v_in"), 1)
                if j == 3 and w.proj is not None:
                    c = w.proj
                    act.wait_ge(sem("hn_mm"), c.o + 1)
                    if due(c.o):
                        act.wait_ge(sem("v_mm"), c.o)
                    act.activation(hT[:, :], mb_ps[:, 0:T], ACT.Identity, scale=cols[c.l][:, 0:1],
                                   bias=cols[c.l][:, 1:2]).then_inc(sem("hT"), 1)
                if j == 5 and w.proj is not None:
                    c = w.proj
                    act.wait_ge(sem("qk_mm"), c.o + 1)
                    if due(c.o):
                        act.wait_ge(sem("rest"), c.o)
                    if due(96 * c.o):
                        act.wait_ge(sem("parts_out"), 96 * c.o)
                    for side in range(2):
                        half = slice(side * T, (side + 1) * T)
                        bias = cols[c.l][:, 2 + side:3 + side]
                        act.activation(qk32[:, half], mb_ps[:, half], ACT.Identity, bias=bias)
                        last = act.activation(parts[:, 0, half], mb_ps[:, half], ACT.Identity, bias=bias)
                    last.then_inc(sem("qk32"), 1)
                if j == 7 and w.post is not None:
                    a = w.post
                    act.wait_ge(sem("ynt_mm"), a.o + 1)
                    if due(a.o):
                        act.wait_ge(sem("wo_mm"), a.o)
                    act.activation(yT[:, :], mb_ps[:, 0:T], ACT.Copy).then_inc(sem("yT"), 1)
                if j == 13 and w.post is not None:
                    a = w.post
                    act.wait_ge(sem("hn2_mm"), a.o + 1)
                    if due(2 * a.o):
                        act.wait_ge(sem("u_mm"), 2 * a.o)
                    act.activation(h2T[:, :], mb_ps[:, 0:T], ACT.Identity, scale=cols[a.l][:, 4:5],
                                   bias=cols[a.l][:, 5:6]).then_inc(sem("h2T"), 1)
                if j == 15 and w.post is not None:
                    a = w.post
                    if due(a.o):
                        act.wait_ge(sem("w2_mm"), a.o)
                    for c in range(NCH):
                        act.wait_ge(sem("u_mm"), 2 * a.o + 1 + c // 2)
                        src = (ma_ps, mb_ps)[c // 2]
                        act.activation(gel[:, c, :], src[:, (c % 2) * T:(c % 2 + 1) * T], ACT.Gelu,
                                       bias=cols[a.l][:, 7 + c:8 + c]).then_inc(sem("gelu"), 1)

        act.wait_ge(sem("setup_in"), 16 * N_LOADS)
        run_steps(act, step)
        scalar_tail(act)

    @block.tensor
    def _(pe):
        pe.wait_ge(sem("setup_in"), 16 * N_LOADS)
        pe.wait_ge(sem("dve_const"), 3)
        pe.wait_ge(sem("bv_wide"), L)
        for l in range(L):
            pe.matmul(ma_ps[:, l * P:(l + 1) * P], yraw[:, l * P:(l + 1) * P], wo[l][:, :],
                      start=True, stop=True).then_inc(sem("bo_mm"), 1)

        def scores(bank, item, h, maxima, masked, transposed):
            rows = slice(0 if masked else ROW_PROD, ROWS if maxima else ROW_MAX)
            for a in range(2):
                b = a if masked else 1 - a
                x, y = (kst, qst) if transposed else (qst, kst)
                last = pe.matmul(bank[:, a, b * P:(b + 1) * P], x[item.p][rows, h, a * P:(a + 1) * P],
                                 y[item.p][rows, h, b * P:(b + 1) * P], start=True, stop=True)
            return last

        def weigh(item, q):
            pe.wait_ge(sem("exp"), 16 * item.o + 4 * q + 4)
            if q == 0:
                if due(item.o):
                    pe.wait_ge(sem("yraw"), item.o)
            s, u = q // 2, q % 2
            for t in range(2):
                for g in range(4):
                    h = 16 * 0 + 8 * s + 4 * u + g
                    last = pe.matmul(pv_ps[32 * g:32 * g + 32, s * T:(s + 1) * T],
                                     vpad[item.p][:, t, 8 * s + 2 * g + u, :],
                                     probs[:, h % 8, t * T:(t + 1) * T],
                                     start=(u == 0 and t == 0), stop=(u == 1 and t == 1),
                                     tile_position=(0, 32 * g), skip_group_check=True)
            last.then_inc(sem("pv_mm"), 1)

        def turn_maxima(item, g):
            c = 2 * item.o + g
            pe.wait_ge(sem("nm_parts"), c + 1)
            if due(c):
                pe.wait_ge(sem("nm_rows"), c)
            pe.transpose(mt_ps[:, g, 0:P], nm_parts[:, g, :, :].rearrange("p a b -> p (a b)"),
                         identb[:, :]).then_inc(sem("nm_mm"), 1)

        def step(w, _):
            for j in range(H):
                if w.cur is not None:
                    k = w.cur
                    if j % 8 == 0:
                        if due(144 * (k.o + 1)):
                            pe.wait_ge(sem(f"stack_in{j // 8}"), 144 * (k.o + 1))
                        if due(16 * (k.o + 1)):
                            pe.wait_ge(sem(f"max_in{j // 8}"), 16 * (k.o + 1))
                    if j == 0:
                        pe.wait_ge(sem("v_in"), k.o + 1)
                    if due(16 * k.o + j - 1):
                        pe.wait_ge(sem("exp"), 16 * k.o + j - 1)
                    scores(st_ps[j % 2], k, j, True, True, True)
                if w.next is not None:
                    k = w.next
                    if j % 8 == 0:
                        if due(144 * (k.o + 1)):
                            pe.wait_ge(sem(f"stack_in{j // 8}"), 144 * (k.o + 1))
                    if due(16 * k.o + j - 1):
                        pe.wait_ge(sem("maxed"), 16 * k.o + j - 1)
                    scores(sm_ps[j % 2], k, j, False, True, False)
                    scores(sm_ps[j % 2], k, j, False, False, False).then_inc(sem("sm_mm"), 1)
                if w.cur is not None:
                    scores(st_ps[j % 2], w.cur, j, True, False, True).then_inc(sem("st_mm"), 1)
                if j == 1 and w.post is not None:
                    weigh(w.post, 3)
                if j == 1 and w.cur is not None:
                    turn_maxima(w.cur, 1)
                if j == 1 and w.next is not None:
                    c = w.next
                    if w.last is not None:
                        pe.wait_ge(sem("gelu"), 4 * w.last.o + 2)
                    else:
                        if due(c.o):
                            pe.wait_ge(sem("v_in"), c.o)
                        if w.post is not None and due(w.post.o):
                            pe.wait_ge(sem("ffn_out"), w.post.o)
                    for t in range(2):
                        last = pe.matmul(ma_ps[:, t * P:(t + 1) * P], hT[:, t * P:(t + 1) * P], wv[c.l][:, :],
                                         start=True, stop=True)
                    last.then_inc(sem("v_mm"), 1)
                if j == 2 and w.last is not None:
                    e = w.last
                    if w.next is not None:
                        pe.wait_ge(sem("v_in"), w.next.o + 1)
                    pe.wait_ge(sem("gelu"), 4 * e.o + 4)
                    for t in range(2):
                        for c in range(NCH):
                            last = pe.matmul(ma_ps[:, t * P:(t + 1) * P], gel[:, c, t * P:(t + 1) * P],
                                             w2[e.l][:, c, :], start=(c == 0), stop=(c == NCH - 1))
                    last.then_inc(sem("w2_mm"), 1)
                if j == 2 and w.proj is not None:
                    c = w.proj
                    if w.last is not None:
                        pe.wait_ge(sem("gelu"), 4 * w.last.o + 4)
                    elif due(c.o):
                        pe.wait_ge(sem("qk32"), c.o)
                    pe.wait_ge(sem("hn"), c.o + 1)
                    for t in range(2):
                        last = pe.transpose(mb_ps[:, t * P:(t + 1) * P], hn[:, t, :], ident[:, :])
                    last.then_inc(sem("hn_mm"), 1)
                if j == 3 and w.post is not None:
                    a = w.post
                    if due(a.o):
                        pe.wait_ge(sem("ffn_out"), a.o)
                    if w.last is None and w.next is not None:
                        pe.wait_ge(sem("v_in"), w.next.o + 1)
                    pe.wait_ge(sem("yraw"), a.o + 1)
                    for n in range(4):
                        m = 2 * (n % 2) + n // 2
                        last = pe.transpose(ma_ps[:, m * P:(m + 1) * P], yraw[:, n * P:(n + 1) * P], ident[:, :])
                    last.then_inc(sem("yt_mm"), 1)
                if j == 4 and w.proj is not None:
                    c = w.proj
                    pe.wait_ge(sem("hT"), c.o + 1)
                    for side, wt in enumerate((wq, wk)):
                        last = pe.matmul(mb_ps[:, side * T:(side + 1) * T], wt[c.l][:, :], hT[:, :], start=True, stop=True)
                    last.then_inc(sem("qk_mm"), 1)
                if j == 5 and w.cur is not None:
                    weigh(w.cur, 0)
                if j == 6 and w.post is not None:
                    a = w.post
                    if w.proj is not None:
                        pe.wait_ge(sem("qk32"), w.proj.o + 1)
                    else:
                        if due(4 * a.o):
                            pe.wait_ge(sem("gelu"), 4 * a.o)
                        if w.next is not None:
                            pe.wait_ge(sem("qk32"), w.next.o + 1)
                    pe.wait_ge(sem("yn"), a.o + 1)
                    yv = yn[:, :, :].rearrange("p (t m) d -> p t (m d)", t=2)
                    for t in range(2):
                        last = pe.transpose(mb_ps[:, t * P:(t + 1) * P], yv[:, t, :], ident[:, :])
                    last.then_inc(sem("ynt_mm"), 1)
                if j == 8 and w.post is not None:
                    a = w.post
                    pe.wait_ge(sem("yT"), a.o + 1)
                    for t in range(2):
                        last = pe.matmul(ma_ps[:, t * P:(t + 1) * P], yT[:, t * P:(t + 1) * P], wo[a.l][:, :],
                                         start=True, stop=True)
                    last.then_inc(sem("wo_mm"), 1)
                if j == 9 and w.cur is not None:
                    weigh(w.cur, 1)
                if j == 9 and w.next is not None:
                    turn_maxima(w.next, 0)
                if j == 12 and w.post is not None:
                    a = w.post
                    pe.wait_ge(sem("hn2"), a.o + 1)
                    for t in range(2):
                        last = pe.transpose(mb_ps[:, t * P:(t + 1) * P], hn2[:, t, :], ident[:, :])
                    last.then_inc(sem("hn2_mm"), 1)
                if j == 13 and w.cur is not None:
                    weigh(w.cur, 2)
                if j == 14 and w.post is not None:
                    a = w.post
                    pe.wait_ge(sem("h2T"), a.o + 1)
                    for m, bank in enumerate((ma_ps, mb_ps)):
                        for c in range(2):
                            last = pe.matmul(bank[:, c * T:(c + 1) * T], w1[a.l][:, (2 * m + c) * P:(2 * m + c + 1) * P],
                                             h2T[:, :], start=True, stop=True)
                        last.then_inc(sem("u_mm"), 1)

        run_steps(pe, step)
        tensor_tail(pe)


_INS = ["L0_attn_" + n for n in ("x", "ln1_g", "ln1_b", "wq", "bq", "wk", "bk", "wv", "bv", "wo", "bo", "ln2_g", "ln2_b",
                                 "w1", "b1", "w2", "b2", "lnf_g", "lnf_b")]
_INS += ["L0_ffn_w_" + n for n in ("router", "gate", "up", "down")]


def kernel(**inputs):
    import concourse.bacc as _bacc
    from concourse.bass_utils import run_bass_kernel_spmd as _run

    nc = _bacc.Bacc("TRN2", target_bir_lowering=False, num_devices=1)
    arrays, aps = {}, {}
    given = {name: np.ascontiguousarray(inputs[name]) for name in _INS}
    given.update({"const_" + k: v for k, v in constants().items()})
    for name, a in given.items():
        arrays[f"in_{name}"] = a
        aps[name] = nc.dram_tensor(f"in_{name}", a.shape, mybir.dt.from_np(a.dtype), kind="ExternalInput").ap()
    out = nc.dram_tensor("out_0", (NB, T, P), F32, kind="ExternalOutput").ap()
    build(nc, aps, out)
    r = _run(nc, [arrays], core_ids=[0])
    return r.results[0]["out_0"]
```

```python
from contextlib import ExitStack

import numpy as np
import concourse.bass as bass
from concourse import mybir

F32 = mybir.dt.float32
BF16 = mybir.dt.bfloat16
U32 = mybir.dt.uint32
ALU = mybir.AluOpType
ACT = mybir.ActivationFunctionType
AX = mybir.AxisListType

P = 128
NB, T = 16, 256
H, HD = 16, 8
L = 2
FF = 512
NCH = FF // P
E, CAP = 32, 160
NT = NB * T // P
HALF = CAP // 2
EPS = 1e-5
SCALE = float(np.float32(1.0) / np.sqrt(HD).astype(np.float32))
BIG = -1e38

ROW_MASK = 0
N_MASK = 43
ROW_PROD = 64
ROW_ALL = 112
ROW_MAX = 113
ROWS = 116
BLOCKS = [(0, 0), (0, 1), (0, 2), (1, 0), (1, 1), (2, 0)]

DUMP = E * CAP
FIRST_LOOP, LAST_LOOP = 4, 13


def constants():
    q = np.arange(T)
    qrows = np.zeros((P, T), np.float32)
    krows = np.zeros((P, T), np.float32)
    for j in range(N_MASK):
        qrows[ROW_MASK + j, [3 * j, P + 1 + 3 * j]] = 1.0
        krows[ROW_MASK + j] = np.where(q < P, np.where(q > 3 * j, BIG, 0.0), np.where(q > P + 1 + 3 * j, BIG, 0.0))
    qrows[ROW_ALL] = (q % 3 == 0) & (q < P)
    krows[ROW_ALL] = np.where(q >= P, BIG, 0.0)
    krows[ROW_MAX:ROW_MAX + 3] = 1.0
    ident = np.eye(P, dtype=np.float32)
    tri = np.triu(np.ones((P, P), np.float32))
    rev = np.tile(E - np.arange(E, dtype=np.float32), (P, 1))
    order = np.arange(P).reshape(2, 2, 4, HD).transpose(0, 2, 1, 3).reshape(-1)
    perm = np.eye(P, dtype=np.float32)[:, order]
    dump = DUMP + np.arange(NT, dtype=np.float32)[None, :] * P + np.arange(P, dtype=np.float32)[:, None]
    return {"qrows": qrows, "krows": krows, "ident": ident, "tri": tri, "rev": rev, "dump": dump, "perm": perm}


class Item:

    def __init__(self, n, o, b, layer, parity):
        self.n, self.o, self.b, self.l, self.p = n, o, b, layer, parity


def item_at(n):
    if n < 0 or n > 2 * NB + 3 or n in (1, 3, 2 * NB, 2 * NB + 2):
        return None
    o = n - sum(1 for hole in (1, 3, 2 * NB, 2 * NB + 2) if hole < n)
    return Item(n, o, n // 2 if n % 2 == 0 else (n - 5) // 2, n % 2, o % 2)


class Step:

    def __init__(self, s=None, i=None, c=0):
        def at(d):
            if i is None:
                return item_at(s + d)
            k = c + d
            b = i + k // 2 if k % 2 == 0 else i + (k - 5) // 2
            return Item(None, 2 * i + (k - 2), b, k % 2, k % 2)
        self.pre = at(3)
        self.raw = self.pre if self.pre is not None and self.pre.l == 0 else None
        self.proj = at(2)
        self.next = at(1)
        self.cur = at(0)
        self.post = at(-1)
        self.last = at(-2)
        self.old = at(-3)
        old, oldest = self.old, at(-4)
        self.final = old if old is not None and old.l == 1 else None
        self.router = oldest if oldest is not None and oldest.l == 1 else None


def build(nc, ins, out):
    ctx = ExitStack()
    with ctx:
        _build(nc, ctx, ins, out)


def _build(nc, ctx, ins, out):
    def sb(name, shape, dt=F32):
        return ctx.enter_context(nc.sbuf_tensor(name, shape, dt))

    def ps(name, shape, dt=F32):
        return ctx.enter_context(nc.psum_tensor(name, shape, dt))

    sems = {}

    def sem(name):
        if name not in sems:
            sems[name] = ctx.enter_context(nc.semaphore(name))
        return sems[name]

    def due(value):
        return not isinstance(value, int) or value > 0

    n_holds = [0]

    def hold(eng, value):
        if value is not None and not isinstance(value, int):
            n_holds[0] += 1
            to = scratch[:, n_holds[0]:n_holds[0] + 1]
            if eng is nc.vector:
                eng.tensor_copy(to, scratch[:, 0:1])
            else:
                eng.tensor_tensor(to, scratch[:, 0:1], scratch[:, 0:1], ALU.add)

    parts_d = [nc.dram_tensor(f"parts_d{p}", (3, 2, HD, H, T), BF16, kind="Internal").ap() for p in range(2)]
    xbuf_d = nc.dram_tensor("xbuf_d", (DUMP + NB * T, P), F32, kind="Internal").ap()
    ybuf_d = nc.dram_tensor("ybuf_d", (DUMP + P, P), F32, kind="Internal").ap()

    XO = sb("x_outer", [P, NT * P])
    XR = sb("x_inner", [P, NT * P])
    qst = [sb(f"q_stack{p}", [P, H, T], BF16) for p in range(2)]
    kst = [sb(f"k_stack{p}", [P, H, T], BF16) for p in range(2)]
    vpad = [sb(f"v_pad{p}", [P, 2, H, 32]) for p in range(2)]
    probs = sb("probs", [P, 8, 2 * T])
    hn = sb("hn", [P, 2, P])
    hT = sb("hT", [P, T])
    qk32 = sb("qk32", [P, 2 * T])
    rest = sb("rest", [P, 2 * T])
    parts = sb("parts", [P, 3, 2 * T], BF16)
    maxes = [sb(f"maxes{p}", [P, H, 2]) for p in range(2)]
    nm_rest = sb("nm_rest", [P, 2, 16])
    nm_parts = sb("nm_parts", [P, 2, 8, 16], BF16)
    nm_rows = sb("nm_rows", [48, 2, P], BF16)
    yraw = sb("yraw", [P, 2 * T])
    rden = sb("rden", [P, 2 * H])
    yn = sb("yn", [P, 2 * H, HD])
    yT = sb("yT", [P, T])
    hn2 = sb("hn2", [P, 2, P])
    h2T = sb("h2T", [P, T])
    gel = sb("gel", [P, NCH, T])
    w_in = gel[:, :, :].rearrange("p k t -> p (k t)").rearrange("p (n c) -> p n c", c=P)
    fin = sb("fin", [P, 2, P])
    bn = {k: sb(f"bn_{k}", [P, 2, 6]) for k in ("raw", "proj", "post", "f1", "f2", "f3")}
    mv = {k: sb(f"mv_{k}", [P, 2, 2]) for k in bn}
    rs = {k: sb(f"rs_{k}", [P, 2, 2]) for k in bn}
    consts = {k: sb(f"c_{k}", [P, v.shape[1]]) for k, v in constants().items()}
    ident = consts["ident"]
    identb = sb("identb", [P, P], BF16)
    trib = sb("trib", [P, P], BF16)
    onesb = sb("onesb", [P, P], BF16)
    eps_mh = sb("eps_mh", [P, 2, 2])
    wq = [sb(f"wq{l}", [P, P]) for l in range(L)]
    wk = [sb(f"wk{l}", [P, P]) for l in range(L)]
    wv = [sb(f"wv{l}", [P, P]) for l in range(L)]
    wo = [sb(f"wo{l}", [P, P]) for l in range(L)]
    w1 = [sb(f"w1{l}", [P, FF]) for l in range(L)]
    w2 = [sb(f"w2{l}", [P, NCH, P]) for l in range(L)]
    cols = sb("cols", [P, 7 + NCH, L])
    bo_row = [sb(f"bo_row{l}", [P, 2, P]) for l in range(L)]
    b2_row = [sb(f"b2_row{l}", [P, 2, P]) for l in range(L)]
    lnf = sb("lnf", [P, 2, P])
    wr = sb("wr", [P, E])
    zero = sb("zero", [P, 512])
    scratch = sb("scratch", [P, 64])

    wgate = sb("wgate", [P, E, P])
    wup = sb("wup", [P, E, P])
    wdown = sb("wdown", [P, E, P])
    logits = sb("logits", [P, NT * E])
    slot_in = sb("slot_in", [P, NT], U32)
    slot_out = sb("slot_out", [P, NT], U32)
    small = {k: sb(f"r_{k}", [P, NT]) for k in ("top", "rev", "sum", "gate", "place", "taken", "slot", "to")}
    bn_out = sb("bn_out", [P, NT, 6])
    mv_out = sb("mv_out", [P, NT, 2])
    rs_out = sb("rs_out", [P, NT, 2])
    shift = sb("shift", [P, NT])
    diff = probs[:, 4:6, :].rearrange("p a b -> p (a b)")
    expd = probs[:, 6:8, :].rearrange("p a b -> p (a b)")
    yg = probs[:, :, :].rearrange("p a (b c) -> p (a b) c", c=P)
    cand = gel[:, :, :].rearrange("p a b -> p (a b)")
    onehot = parts[:, 0:2, :].rearrange("p a b -> p (a b)")
    xeT = yraw[:, :].rearrange("p (a b) -> p a b", a=2)[:, :, 0:CAP]
    sg = qk32[:, :].rearrange("p (a b) -> p a b", a=2)[:, :, 0:CAP]
    hid = rest[:, :].rearrange("p (a b) -> p a b", a=2)[:, :, 0:CAP]
    yout = vpad[0][0:HALF, :, :, :].rearrange("p t h c -> p (t h c)").rearrange("p (m n c) -> p m n c", m=4, n=2)

    st_ps = [ps(f"st_ps{i}", [P, 2, T]) for i in range(2)]
    sm_ps = [ps(f"sm_ps{i}", [P, 2, T]) for i in range(2)]
    pv_ps = ps("pv_ps", [P, 2 * T])
    mt_ps = ps("mt_ps", [P, 2, 512], BF16)
    ma_ps = ps("ma_ps", [P, 512])
    mb_ps = ps("mb_ps", [P, 512])

    block = ctx.enter_context(nc.Block())

    def x_of(buf, b):
        if isinstance(b, int):
            return buf[:, b * 2 * P:(b + 1) * 2 * P]
        return buf[:, bass.ds(b * (2 * P), 2 * P)]

    def tiles(ap):
        return ap.rearrange("p (t c) -> p t c", t=2)

    def tile_of(buf, b, t):
        if isinstance(b, int):
            return buf[:, (2 * b + t) * P:(2 * b + t + 1) * P]
        return buf[:, bass.ds(b * (2 * P) + t * P, P)]

    def run_steps(eng, step):
        for s in range(-3, 2 * FIRST_LOOP):
            step(Step(s), None)
        with eng.Fori(FIRST_LOOP, LAST_LOOP + 1) as i:
            for c in range(2):
                step(Step(i=i, c=c), (i, c))
        for s in range(2 * LAST_LOOP + 2, 2 * NB + 8):
            step(Step(s), None)

    N_LOADS = len(consts) + L * (6 + 2 + 1 + 4) + 5 + 3


    def xt_tile(n):
        return XR[:, n * P:(n + 1) * P]

    def expert_rows(q):
        buf = (qst[0], qst[1], kst[0], kst[1])[q]
        return buf[0:HALF, :, :].rearrange("p h t -> p (h t)").bitcast(F32).rearrange("p (n c) -> p n c", c=P)

    def sync_tail(sp):
        sp.wait_ge(sem("scattered"), 16 * NT)
        for q in range(4):
            rows = xbuf_d[q * 8 * CAP:(q + 1) * 8 * CAP, :].rearrange("(n p) c -> p n c", p=HALF)
            sp.dma_start(expert_rows(q), rows).then_inc(sem(f"buf_in{q}"), 16)
        for e in range(E):
            sp.wait_ge(sem("y_out"), e + 1)
            rows = ybuf_d[e * CAP:(e + 1) * CAP, :].rearrange("(n p) c -> p n c", p=HALF)
            sp.dma_start(rows, yout[:, e % 4, :, :]).then_inc(sem(f"y_stored{e % 4}"), 16)
        ov = out.rearrange("b (t p) c -> p (b t) c", p=P)
        for g in range(NT // 4):
            sp.wait_ge(sem("result"), g + 1)
            sp.dma_start(ov[:, 4 * g:4 * g + 4, :], XO[:, g * 4 * P:(g + 1) * 4 * P].rearrange("p (n c) -> p n c", c=P)
                         ).then_inc(sem("stored"), 16)
        sp.wait_ge(sem("stored"), 16 * (NT // 4))

    def pool_tail(pool):
        pool.wait_ge(sem("dram_zero"), 16 * (DUMP // (4 * P) + 1))
        pool.wait_ge(sem("slots"), 1)
        pool.wait_ge(sem("xt"), NB)
        for n in range(NT):
            pool.indirect_dma_start(xbuf_d, bass.IndirectOffsetOnAxis(ap=slot_in[:, n:n + 1], axis=0),
                                    xt_tile(n), None).then_inc(sem("scattered"), 16)
        for m in range(4):
            pool.wait_ge(sem(f"y_stored{m}"), 16 * (E // 4))
        for n in range(NT):
            pool.indirect_dma_start(yg[:, n, :], None, ybuf_d,
                                    bass.IndirectOffsetOnAxis(ap=slot_out[:, n:n + 1], axis=0)).then_inc(sem(f"y_in{n // 4}"), 16)
        for g in range(NT // 4):
            s = slice(4 * g, 4 * g + 4)
            pool.wait_ge(sem("mv_out"), 4 * g + 4)
            pool.tensor_tensor(rs_out[:, s, 0], mv_out[:, s, 1], eps_mh[:, 0:1, 0].to_broadcast([P, 4]), ALU.add).then_inc(sem("ve_out"), 1)
            pool.wait_ge(sem("ve_out"), g + 1)
            pool.tensor_tensor(rs_out[:, s, 1], rs_out[:, s, 0], eps_mh[:, 0:1, 1].to_broadcast([P, 4]), ALU.pow).then_inc(sem("rs_out"), 1)
        for g in range(NT // 4):
            s = slice(g * 4 * P, (g + 1) * 4 * P)
            pool.wait_ge(sem("normed"), g + 1)
            pool.tensor_tensor(XO[:, s], XO[:, s], XR[:, s], ALU.add).then_inc(sem("result"), 1)

    def scalar_tail(act):
        for g in range(NT // 4):
            act.wait_ge(sem("rt_mm"), g + 1)
            if due(g - 3):
                act.wait_ge(sem("lg_mm"), g - 3)
            act.activation(probs[:, g % 4, :], (ma_ps, mb_ps)[g % 2][:, :], ACT.Copy).then_inc(sem("rt_in"), 1)
        act.wait_ge(sem("lg_diff"), 1)
        act.activation(expd[:, :], diff[:, :], ACT.Exp).then_inc(sem("expd"), 1)
        for e in range(E):
            act.wait_ge(sem("et_mm"), e + 1)
            if due(e - 1):
                act.wait_ge(sem("gu_mm"), e - 1)
            act.activation(xeT[:, e % 2, :], st_ps[e % 2][:, 0, 0:CAP], ACT.Copy).then_inc(sem("xeT"), 1)
            act.wait_ge(sem("gu_mm"), e + 1)
            if due(e - 1):
                act.wait_ge(sem("act"), e - 1)
            act.activation(sg[:, e % 2, :], sm_ps[e % 2][:, 0, 0:CAP], ACT.Silu).then_inc(sem("silu"), 1)
        for n in range(NT):
            act.wait_ge(sem("shift"), n // 4 + 1)
            last = act.activation(xt_tile(n), xt_tile(n), ACT.Identity, scale=rs_out[:, n, 1:2], bias=shift[:, n:n + 1])
            if n % 4 == 3:
                last.then_inc(sem("normed"), 1)

    def vector_tail(dve):
        lg = logits[:, :].rearrange("p (n e) -> p n e", e=E)
        df = diff[:, :].rearrange("p (n e) -> p n e", e=E)
        ex = expd[:, :].rearrange("p (n e) -> p n e", e=E)
        cd = cand[:, :].rearrange("p (n e) -> p n e", e=E)
        oh = onehot[:, :].rearrange("p (n e) -> p n e", e=E)

        def wide(ap):
            return ap.rearrange("p (n o) -> p n o", o=1).to_broadcast([P, NT, E])

        n_link = [0]

        def link(ins):
            n_link[0] += 1
            ins.then_inc(sem("route"), 1)
            dve.wait_ge(sem("route"), n_link[0])

        for m in range(2):
            dve.wait_ge(sem("lg_mm"), 4 * m + 4)
            dve.tensor_copy(logits[:, 512 * m:512 * m + 512], st_ps[m][:, :, :].rearrange("p a b -> p (a b)")).then_inc(sem("lg"), 1)
        dve.wait_ge(sem("lg"), 2)
        link(dve.tensor_reduce(small["top"][:, :], lg, AX.X, ALU.max))
        dve.tensor_tensor(df, lg, wide(small["top"][:, :]), ALU.subtract).then_inc(sem("lg_diff"), 1)
        dve.wait_ge(sem("lg_diff"), 1)
        link(dve.scalar_tensor_tensor(out=cd, in0=df, scalar=0.0,
                                      in1=consts["rev"][:, :].rearrange("p (o e) -> p o e", o=1).to_broadcast([P, NT, E]),
                                      op0=ALU.is_ge, op1=ALU.mult))
        link(dve.tensor_reduce(small["rev"][:, :], cd, AX.X, ALU.max))
        dve.tensor_tensor(oh, cd, wide(small["rev"][:, :]), ALU.is_equal).then_inc(sem("onehot"), 1)
        dve.wait_ge(sem("expd"), 1)
        link(dve.tensor_reduce(small["sum"][:, :], ex, AX.X, ALU.add))
        link(dve.reciprocal(small["gate"][:, :], small["sum"][:, :]))
        dve.wait_ge(sem("tot_mm"), 2)
        for m, bank in enumerate((ma_ps, mb_ps)):
            link(dve.tensor_copy(diff[:, 512 * m:512 * m + 512], bank[:, :]))
        a, b, d = diff, expd, 1
        while d < NT:
            link(dve.tensor_tensor(b[:, d * E:], a[:, d * E:], a[:, 0:(NT - d) * E], ALU.add))
            link(dve.tensor_copy(b[:, 0:d * E], a[:, 0:d * E]))
            a, b, d = b, a, 2 * d
        dve.wait_ge(sem("inc_mm"), 2)
        for m, bank in enumerate(sm_ps):
            src = bank[:, :, :].rearrange("p a b -> p (a b)")
            if m == 0:
                link(dve.tensor_copy(logits[:, 0:E], src[:, 0:E]))
                link(dve.tensor_tensor(logits[:, E:512], src[:, E:512], a[:, 0:512 - E], ALU.add))
            else:
                link(dve.tensor_tensor(logits[:, 512:1024], src, a[:, 512 - E:1024 - E], ALU.add))
        link(dve.tensor_tensor(logits[:, :], logits[:, :], onehot[:, :], ALU.mult))
        link(dve.tensor_reduce(small["place"][:, :], lg, AX.X, ALU.add))
        link(dve.tensor_single_scalar(small["taken"][:, :], small["place"][:, :], float(CAP), ALU.is_le))
        link(dve.scalar_tensor_tensor(out=small["slot"][:, :], in0=small["rev"][:, :], scalar=-float(CAP),
                                      in1=small["place"][:, :], op0=ALU.mult, op1=ALU.add))
        link(dve.tensor_scalar(small["slot"][:, :], small["slot"][:, :], float(E * CAP - 1), None, ALU.add))
        link(dve.tensor_tensor(small["to"][:, :], small["slot"][:, :], consts["dump"][:, :], ALU.subtract))
        link(dve.tensor_tensor(small["to"][:, :], small["to"][:, :], small["taken"][:, :], ALU.mult))
        link(dve.tensor_tensor(slot_in[:, :], small["to"][:, :], consts["dump"][:, :], ALU.add))
        link(dve.tensor_scalar(small["slot"][:, :], small["slot"][:, :], -float(DUMP), None, ALU.add))
        link(dve.tensor_tensor(small["slot"][:, :], small["slot"][:, :], small["taken"][:, :], ALU.mult))
        dve.tensor_scalar(slot_out[:, :], small["slot"][:, :], float(DUMP), None, ALU.add).then_inc(sem("slots"), 1)
        for e in range(E):
            dve.wait_ge(sem("silu"), e + 1)
            if due(e - 1):
                dve.wait_ge(sem("ye_mm"), e - 1)
            dve.tensor_tensor(hid[:, e % 2, :], sm_ps[e % 2][:, 1, 0:CAP], sg[:, e % 2, :], ALU.mult).then_inc(sem("act"), 1)
            if e >= 1:
                take_y(dve, e - 1)
        take_y(dve, E - 1)
        for g in range(NT // 4):
            for n in range(4 * g, 4 * g + 4):
                dve.wait_ge(sem(f"y_in{g}"), 64)
                dve.scalar_tensor_tensor(out=xt_tile(n), in0=yg[:, n, :], scalar=small["gate"][:, n:n + 1], in1=xt_tile(n),
                                         op0=ALU.mult, op1=ALU.add).then_inc(sem("z"), 1)
            for n in range(4 * g, 4 * g + 4):
                dve.wait_ge(sem("z"), n + 1)
                dve.bn_stats(bn_out[:, n, :], xt_tile(n)).then_inc(sem("bn_out"), 1)
            for n in range(4 * g, 4 * g + 4):
                dve.wait_ge(sem("bn_out"), n + 1)
                dve.bn_aggr(mv_out[:, n, :], bn_out[:, n, :]).then_inc(sem("mv_out"), 1)
            if g >= 1:
                minus_mean(dve, g - 1)
        minus_mean(dve, NT // 4 - 1)

    def minus_mean(dve, g):
        s = slice(4 * g, 4 * g + 4)
        dve.wait_ge(sem("rs_out"), g + 1)
        dve.scalar_tensor_tensor(out=shift[:, s], in0=mv_out[:, s, 0], scalar=-1.0, in1=rs_out[:, s, 1],
                                 op0=ALU.mult, op1=ALU.mult).then_inc(sem("shift"), 1)

    def take_y(dve, e):
        dve.wait_ge(sem("ye_mm"), e + 1)
        if due(e // 4):
            dve.wait_ge(sem(f"y_stored{e % 4}"), 16 * (e // 4))
        dve.tensor_copy(yout[:, e % 4, :, :], (ma_ps, mb_ps)[e % 2][0:HALF, 0:2 * P].rearrange("p (n c) -> p n c", n=2)
                        ).then_inc(sem("y_out"), 1)

    def tensor_tail(pe):
        pe.wait_ge(sem("xt"), NB)
        pe.wait_ge(sem("exp"), 16 * 2 * NB)
        pe.wait_ge(sem("maxed"), 16 * 2 * NB)
        pe.wait_ge(sem("ffn_out"), 2 * NB)

        def route(g):
            pe.wait_ge(sem("rt_in"), g + 1)
            for n in range(4 * g, 4 * g + 4):
                m = n % 16
                last = pe.matmul(st_ps[n // 16][:, m // 8, (m % 8) * E:(m % 8 + 1) * E], probs[:, g % 4, (n % 4) * P:(n % 4 + 1) * P],
                                 wr[:, :], start=True, stop=True)
            last.then_inc(sem("lg_mm"), 1)

        for g in range(NT // 4):
            if due(g - 1):
                pe.wait_ge(sem("rt_in"), g - 1)
            if g == 0:
                pe.wait_ge(sem("gelu"), 4 * 2 * NB)
            for n in range(4):
                last = pe.transpose((ma_ps, mb_ps)[g % 2][:, n * P:(n + 1) * P], xt_tile(4 * g + n), ident[:, :])
            last.then_inc(sem("rt_mm"), 1)
            if g >= 1:
                route(g - 1)
        route(NT // 4 - 1)
        pe.wait_ge(sem("onehot"), 1)
        pe.wait_ge(sem("rt_in"), NT // 4)
        for m in range(2):
            pe.matmul(sm_ps[m][:, :, :].rearrange("p a b -> p (a b)"), trib[:, :], onehot[:, 512 * m:512 * m + 512],
                      start=True, stop=True).then_inc(sem("inc_mm"), 1)
        for m, bank in enumerate((ma_ps, mb_ps)):
            pe.matmul(bank[:, :], onesb[:, :], onehot[:, 512 * m:512 * m + 512], start=True, stop=True).then_inc(sem("tot_mm"), 1)
        pe.wait_ge(sem("experts_in"), 48)
        pe.wait_ge(sem("slots"), 1)

        def turn(e):
            if e % 8 == 0:
                pe.wait_ge(sem(f"buf_in{e // 8}"), 16)
            if due(e - 1):
                pe.wait_ge(sem("xeT"), e - 1)
            for a in range(2):
                last = pe.transpose(st_ps[e % 2][:, 0, a * HALF:(a + 1) * HALF], expert_rows(e // 8)[:, 2 * (e % 8) + a, :],
                                    ident[0:HALF, 0:HALF])
            last.then_inc(sem("et_mm"), 1)

        def down(e):
            pe.wait_ge(sem("act"), e + 1)
            if due(e - 1):
                pe.wait_ge(sem("y_out"), e - 1)
            for a in range(2):
                last = pe.matmul((ma_ps, mb_ps)[e % 2][0:HALF, a * P:(a + 1) * P], hid[:, e % 2, a * HALF:(a + 1) * HALF],
                                 wdown[:, e, :], start=True, stop=True)
            last.then_inc(sem("ye_mm"), 1)

        turn(0)
        for e in range(E):
            if e + 1 < E:
                turn(e + 1)
            pe.wait_ge(sem("xeT"), e + 1)
            if due(e - 1):
                pe.wait_ge(sem("act"), e - 1)
            for k, w in enumerate((wgate, wup)):
                last = pe.matmul(sm_ps[e % 2][:, k, 0:CAP], w[:, e, :], xeT[:, e % 2, :], start=True, stop=True)
            last.then_inc(sem("gu_mm"), 1)
            if e >= 1:
                down(e - 1)
        down(E - 1)

    @block.sync
    def _(sp):
        xv = ins["L0_attn_x"].rearrange("b (t p) c -> p (b t) c", p=P)
        xo = XO[:, :].rearrange("p (n c) -> p n c", c=P)
        sp.dma_start(xo[:, 0:2, :], xv[:, 0:2, :]).then_inc(sem("x_first"), 16)
        loads = []
        for k in consts:
            loads.append((consts[k][:, :], ins["const_" + k]))
        for n, name in ((0, "ln1_g"), (1, "ln1_b"), (4, "ln2_g"), (5, "ln2_b"), (6, "bv")):
            loads.append((cols[:, n, :].rearrange("p (l o) -> p l o", o=1), ins["L0_attn_" + name].rearrange("l (p o) -> p l o", o=1)))
        for l in range(L):
            row = lambda name: ins["L0_attn_" + name][l:l + 1, :].to_broadcast([P, P])
            for n, name in ((2, "bq"), (3, "bk")):
                loads.append((cols[:, n, l:l + 1], ins["L0_attn_" + name][l].rearrange("(h d o) -> d h o", h=H, o=1)))
            for n, name in enumerate(("wq", "wk", "wv", "wo")):
                loads.append((w_in[:, 4 * l + n, :], ins["L0_attn_" + name][l]))
            loads += [(w1[l][:, :], ins["L0_attn_w1"][l]),
                      (w2[l][:, :, :], ins["L0_attn_w2"][l].rearrange("(k p) n -> p k n", p=P)),
                      (cols[:, 7:7 + NCH, l:l + 1], ins["L0_attn_b1"][l].rearrange("(k p o) -> p k o", p=P, o=1))]
            for t in range(2):
                loads.append((bo_row[l][:, t, :], row("bo")))
                loads.append((b2_row[l][:, t, :], row("b2")))
        loads.append((lnf[:, 0, :], ins["L0_attn_lnf_g"].rearrange("(o c) -> o c", o=1).to_broadcast([P, P])))
        loads.append((lnf[:, 1, :], ins["L0_attn_lnf_b"].rearrange("(o c) -> o c", o=1).to_broadcast([P, P])))
        loads.append((wr[:, :], ins["L0_ffn_w_router"]))
        with nc.allow_non_contiguous_dma(reason="a vector goes to one element a partition"):
            for dst, src in loads:
                sp.dma_start(dst, src).then_inc(sem("setup_in"), 16)
        assert len(loads) == N_LOADS, len(loads)
        sp.dma_start(xo[:, 2:, :], xv[:, 2:, :]).then_inc(sem("x_rest"), 16)
        for w, name in ((wgate, "gate"), (wup, "up"), (wdown, "down")):
            sp.dma_start(w[:, :, :], ins["L0_ffn_w_" + name].rearrange("e h f -> h e f")).then_inc(sem("experts_in"), 16)
        sp.wait_ge(sem("zeroed"), 1)
        for n in range(DUMP // (P * 4)):
            sp.dma_start(xbuf_d[n * 4 * P:(n + 1) * 4 * P, :].rearrange("(p r) c -> p (r c)", p=P),
                         zero[:, :]).then_inc(sem("dram_zero"), 16)
        sp.dma_start(ybuf_d[DUMP:DUMP + P, :], zero[:, 0:P]).then_inc(sem("dram_zero"), 16)

        def read_stack(item, g):
            hs = slice(8 * g, 8 * g + 8)
            d = parts_d[item.p]
            sp.wait_ge(sem("stack_const"), 1)
            if g == 0:
                sp.wait_ge(sem("parts_out"), 16 * item.o + 16)
            if (g == 1 or isinstance(item.o, int)) and due(16 * item.o - 32 + 8 * g + 8):
                sp.wait_ge(sem("st_mm"), 16 * item.o - 32 + 8 * g + 8)
            for n, m, a in ((0, 3, 0), (3, 2, 1), (5, 1, 2)):
                rows = slice(ROW_PROD + 8 * n, ROW_PROD + 8 * (n + m))
                q = d[a, 0:1][:, :, hs, :].rearrange("n d h t -> n d (h t)")
                sp.dma_start(qst[item.p][rows, hs, :], q.to_broadcast([m, HD, 8 * T])).then_inc(sem(f"stack_in{g}"), 16)
                k = d[0:m, 1][:, :, hs, :].rearrange("n d h t -> n d (h t)")
                sp.dma_start(kst[item.p][rows, hs, :], k).then_inc(sem(f"stack_in{g}"), 16)

        def max_rows(item, g):
            sp.wait_ge(sem("nm_rows"), 2 * item.o + g + 1)
            sp.dma_start(qst[item.p][ROW_MAX:ROW_MAX + 3, 8 * g:8 * g + 8, :],
                         nm_rows[:, g, :]).then_inc(sem(f"max_in{g}"), 16)

        def step(w, _):
            if w.next is not None:
                read_stack(w.next, 1)
            if w.cur is not None:
                max_rows(w.cur, 1)
            if w.proj is not None:
                c = w.proj
                if isinstance(c.o, int):
                    if due(96 * (c.o - 1)):
                        sp.wait_ge(sem("stack_in1"), 96 * (c.o - 1))
                sp.wait_ge(sem("parts"), c.o + 1)
                sp.dma_start(parts_d[c.p].rearrange("a s d h t -> (d h) (a s) t"),
                             parts[:, :, :].rearrange("p a (s t) -> p (a s) t", s=2)).then_inc(sem("parts_out"), 16)
            if w.next is not None:
                max_rows(w.next, 0)
            if w.proj is not None:
                read_stack(w.proj, 0)

        run_steps(sp, step)
        sync_tail(sp)

    @block.gpsimd
    def _(pool):
        pool.memset(zero[:, :], 0.0).then_inc(sem("zeroed"), 1)
        pool.memset(eps_mh[:, :, 0:1], EPS).then_inc(sem("eps"), 1)
        pool.memset(eps_mh[:, :, 1:2], -0.5).then_inc(sem("eps"), 1)
        for p in range(2):
            pool.memset(vpad[p][:, :, :, :], 0.0).then_inc(sem("v_zero"), 1)
        pool.wait_ge(sem("v_zero"), 2)
        for p in range(2):
            for u in range(2):
                pool.memset(vpad[p][:, :, :, :].rearrange("p t (s u) c -> p (t s) u c", u=2)[:, :, u, 16 + u:17 + u],
                            1.0).then_inc(sem("v_ones"), 1)
        pool.wait_ge(sem("eps"), 2)
        pool.wait_ge(sem("scratch"), 1)

        def rstd(key, o, count):
            pool.wait_ge(sem(f"mv_{key}"), count)
            pool.tensor_tensor(rs[key][:, :, 0:1], mv[key][:, :, 1:2], eps_mh[:, :, 0:1], ALU.add).then_inc(sem(f"ve_{key}"), 1)
            pool.wait_ge(sem(f"ve_{key}"), o + 1)
            pool.tensor_tensor(rs[key][:, :, 1:2], rs[key][:, :, 0:1], eps_mh[:, :, 1:2], ALU.pow).then_inc(sem(f"rs_{key}"), 1)

        def normalize(key, o, count, dst, src, done):
            rstd(key, o, count)
            pool.tensor_tensor(dst, src, mv[key][:, :, 0:1].to_broadcast([P, 2, P]), ALU.subtract).then_inc(sem(f"sub_{key}"), 1)
            pool.wait_ge(sem(f"sub_{key}"), o + 1)
            pool.wait_ge(sem(f"rs_{key}"), o + 1)
            hold(pool, o)
            pool.tensor_tensor(dst, dst, rs[key][:, :, 1:2].to_broadcast([P, 2, P]), ALU.mult).then_inc(sem(done), 1)

        def step(w, _):
            if w.router is not None:
                f = w.router.b
                normalize("f3", f, 2 * f + 2, tiles(x_of(XR, f)), tiles(x_of(XO, f)), "xt")
            if w.final is not None:
                f = w.final.b
                normalize("f1", f, 2 * f + 2, fin[:, :, :], tiles(x_of(XR, f)), "f1_norm")
                pool.wait_ge(sem("f1_norm"), f + 1)
                pool.tensor_tensor(fin[:, :, :], fin[:, :, :], lnf[:, 0:1, :].to_broadcast([P, 2, P]), ALU.mult).then_inc(sem("f1_g"), 1)
                pool.wait_ge(sem("f1_g"), f + 1)
                pool.tensor_tensor(fin[:, :, :], fin[:, :, :], lnf[:, 1:2, :].to_broadcast([P, 2, P]), ALU.add).then_inc(sem("f1_b"), 1)
            if w.proj is not None:
                o = w.proj.o
                pool.wait_ge(sem("qk32"), o + 1)
                if due(o):
                    pool.wait_ge(sem("part1"), o)
                pool.tensor_tensor(rest[:, :], qk32[:, :], parts[:, 0, :], ALU.subtract).then_inc(sem("rest"), 1)
            if w.post is not None:
                a = w.post
                pool.wait_ge(sem("setup_bo"), L)
                pool.tensor_tensor(tiles(x_of(XR, a.b)), tiles(x_of(XR, a.b)), bo_row[a.l][:, :, :], ALU.add).then_inc(sem("bo_add"), 1)
            if w.proj is not None:
                pool.wait_ge(sem("part1"), w.proj.o + 1)
                pool.tensor_tensor(parts[:, 2, :], rest[:, :], parts[:, 1, :], ALU.subtract).then_inc(sem("parts"), 1)
            if w.final is not None:
                f = w.final.b
                normalize("f2", f, 2 * f + 2, fin[:, :, :], fin[:, :, :], "f2_norm")
                pool.wait_ge(sem("f2_norm"), f + 1)
                hold(pool, f)
                pool.tensor_tensor(tiles(x_of(XO, f)), tiles(x_of(XO, f)), fin[:, :, :], ALU.add).then_inc(sem("x_attn"), 1)
            if w.raw is not None:
                r = w.raw.b
                normalize("raw", r, 2 * r + 2, tiles(x_of(XR, r)), tiles(x_of(XO, r)), "x_inner")
            if w.pre is not None:
                o = w.pre.o
                if due(o):
                    pool.wait_ge(sem("hn_mm"), o)
                normalize("proj", o, 2 * o + 2, hn[:, :, :], tiles(x_of(XR, w.pre.b)), "hn")
            if w.post is not None:
                a = w.post
                if due(a.o):
                    pool.wait_ge(sem("hn2_mm"), a.o)
                normalize("post", a.o, 2 * a.o + 2, hn2[:, :, :], tiles(x_of(XR, a.b)), "hn2")
                pool.tensor_tensor(tiles(x_of(XR, a.b)), tiles(x_of(XR, a.b)), b2_row[a.l][:, :, :], ALU.add).then_inc(sem("b2_add"), 1)

        run_steps(pool, step)
        pool_tail(pool)

    @block.vector
    def _(dve):
        dve.wait_ge(sem("setup_in"), 16 * N_LOADS)
        dve.tensor_copy(identb[:, :], ident[:, :]).then_inc(sem("dve_const"), 1)
        dve.tensor_copy(trib[:, :], consts["tri"][:, :]).then_inc(sem("dve_const"), 1)
        dve.memset(onesb[:, :], 1.0).then_inc(sem("dve_const"), 1)
        dve.memset(scratch[:, :], 0.0).then_inc(sem("scratch"), 1)
        dve.memset(nm_parts[:, :, :, :], 0.0).then_inc(sem("scratch"), 1)
        dve.wait_ge(sem("scratch"), 2)
        for l in range(L):
            for n, w in ((0, wq), (1, wk)):
                dve.tensor_copy(w[l][:, :].rearrange("p (d h) -> p d h", h=H),
                                w_in[:, 4 * l + n, :].rearrange("p (h d) -> p d h", h=H)).then_inc(sem("w_order"), 1)
            for s in range(2):
                half = slice(64 * s, 64 * s + 64)
                dve.tensor_copy(wv[l][:, half].rearrange("p (g u d) -> p g u d", g=4, u=2),
                                w_in[:, 4 * l + 2, half].rearrange("p (u g d) -> p g u d", g=4, u=2)).then_inc(sem("w_order"), 1)
        for l in range(L):
            dve.tensor_copy(yraw[:, l * P:(l + 1) * P], cols[:, 6, l:l + 1].to_broadcast([P, P])).then_inc(sem("bv_wide"), 1)
        for p in range(2):
            for buf, key in ((qst, "qrows"), (kst, "krows")):
                for h in range(0, H, 4):
                    last = dve.tensor_copy(buf[p][0:ROWS, h:h + 4, :],
                                           consts[key][0:ROWS, :].rearrange("p (o t) -> p o t", o=1).to_broadcast([ROWS, 4, T]))
        last.then_inc(sem("stack_const"), 1)
        for l in range(L):
            dve.wait_ge(sem("bo_mm"), L)
            dve.tensor_tensor(bo_row[l][:, :, :], bo_row[l][:, :, :], ma_ps[:, l * P:(l + 1) * P].rearrange(
                "p (o c) -> p o c", o=1).to_broadcast([P, 2, P]), ALU.add).then_inc(sem("setup_bo"), 1)

        for l in range(L):
            dve.wait_ge(sem("wo_order_mm"), L)
            dve.tensor_copy(wo[l][:, :], mb_ps[:, l * P:(l + 1) * P]).then_inc(sem("w_order"), 1)

        def stats(key, buf, b):
            hold(dve, b)
            for t in range(2):
                src = buf[:, t, :] if b is None else tile_of(buf, b, t)
                dve.bn_stats(bn[key][:, t, :], src).then_inc(sem(f"bn_{key}"), 1)

        def aggregate(key, o):
            dve.wait_ge(sem(f"bn_{key}"), 2 * o + 2)
            hold(dve, o)
            for t in range(2):
                dve.bn_aggr(mv[key][:, t, :], bn[key][:, t, :]).then_inc(sem(f"mv_{key}"), 1)

        def minus_max(item, g):
            c = 2 * item.o + g
            m = maxes[item.p][:, 8 * g:8 * g + 8, :].rearrange("p h t -> p (h t)")
            dve.wait_ge(sem("maxed"), 16 * item.o + 8 * g + 8)
            if due(c - 1):
                dve.wait_ge(sem("nm_mm"), c - 1)
            n = nm_parts[:, g]
            dve.tensor_scalar(n[:, 0, :], m, -1.0, None, ALU.mult).then_inc(sem("nm0"), 1)
            dve.wait_ge(sem("nm0"), c + 1)
            dve.scalar_tensor_tensor(out=nm_rest[:, 0, :], in0=m, scalar=-1.0, in1=n[:, 0, :],
                                     op0=ALU.mult, op1=ALU.subtract).then_inc(sem("nm1"), 1)
            dve.wait_ge(sem("nm1"), c + 1)
            dve.tensor_copy(n[:, 1, :], nm_rest[:, 0, :]).then_inc(sem("nm2"), 1)
            dve.wait_ge(sem("nm2"), c + 1)
            dve.tensor_tensor(n[:, 2, :], nm_rest[:, 0, :], n[:, 1, :], ALU.subtract).then_inc(sem("nm_parts"), 1)

        def minus_max_rows(item, g):
            c = 2 * item.o + g
            dve.wait_ge(sem("nm_mm"), c + 1)
            if due(16 * item.o):
                dve.wait_ge(sem(f"max_in{g}"), 16 * item.o)
            dve.tensor_copy(nm_rows[:, g, :], mt_ps[0:48, g, 0:P]).then_inc(sem("nm_rows"), 1)

        def step(w, _):
            for j in range(H):
                if w.next is not None:
                    o = w.next.o
                    dve.wait_ge(sem("sm_mm"), 16 * o + j + 1)
                    dve.tensor_reduce(maxes[w.next.p][:, j, :], sm_ps[j % 2][:, :, :], AX.X, ALU.max).then_inc(sem("maxed"), 1)
                if j == 0 and w.cur is not None:
                    minus_max(w.cur, 1)
                if j == 1 and w.router is not None:
                    f = w.router.b
                    dve.wait_ge(sem("x_attn"), f + 1)
                    if due(f):
                        dve.wait_ge(sem("sub_f3"), f)
                    stats("f3", XO, f)
                    aggregate("f3", f)
                if j == 1 and w.final is not None:
                    f = w.final.b
                    dve.wait_ge(sem("ffn_out"), w.final.o + 1)
                    if due(f):
                        dve.wait_ge(sem("sub_f1"), f)
                    stats("f1", XR, f)
                    aggregate("f1", f)
                if j == 3 and w.cur is not None:
                    minus_max_rows(w.cur, 1)
                if j == 2 and w.raw is not None:
                    r = w.raw.b
                    if isinstance(r, int) and r == 0:
                        dve.wait_ge(sem("x_first"), 16)
                    elif isinstance(r, int) and r == 1:
                        dve.wait_ge(sem("x_rest"), 16)
                    if due(r):
                        dve.wait_ge(sem("sub_raw"), r)
                    stats("raw", XO, r)
                    aggregate("raw", r)
                if j == 4 and w.post is not None:
                    a = w.post
                    dve.wait_ge(sem("yt_mm"), a.o + 1)
                    src = ma_ps[:, :].rearrange("p (n r) -> p n r", r=32)
                    dve.reciprocal(rden[:, :].rearrange("p (n u) -> p n u", u=2), src[:, :, 16:18]).then_inc(sem("rden"), 1)
                    dve.wait_ge(sem("rden"), a.o + 1)
                    if due(a.o):
                        dve.wait_ge(sem("ynt_mm"), a.o)
                    dve.tensor_tensor(yn[:, :, :].rearrange("p (n u) d -> p n u d", u=2),
                                      src[:, :, 0:16].rearrange("p n (u d) -> p n u d", u=2),
                                      rden[:, :].rearrange("p (n u o) -> p n u o", u=2, o=1).to_broadcast([P, H, 2, HD]),
                                      ALU.mult).then_inc(sem("yn"), 1)
                if j == 7 and w.proj is not None:
                    dve.wait_ge(sem("rest"), w.proj.o + 1)
                    dve.tensor_copy(parts[:, 1, :], rest[:, :]).then_inc(sem("part1"), 1)
                if j == 8 and w.next is not None:
                    minus_max(w.next, 0)
                if j == 8 and w.final is not None:
                    f = w.final.b
                    dve.wait_ge(sem("f1_b"), f + 1)
                    if due(f):
                        dve.wait_ge(sem("sub_f2"), f)
                    stats("f2", fin, None)
                    aggregate("f2", f)
                if j == 10 and w.next is not None:
                    minus_max_rows(w.next, 0)
            if w.last is not None:
                e = w.last
                dve.wait_ge(sem("w2_mm"), e.o + 1)
                dve.wait_ge(sem("b2_add"), e.o + 1)
                dve.tensor_tensor(x_of(XR, e.b), ma_ps[:, 0:2 * P], x_of(XR, e.b), ALU.add).then_inc(sem("ffn_out"), 1)
            if w.pre is not None:
                if w.pre.l == 0:
                    dve.wait_ge(sem("x_inner"), w.pre.b + 1)
                elif w.last is not None:
                    dve.wait_ge(sem("ffn_out"), w.last.o + 1)
                if due(w.pre.o):
                    dve.wait_ge(sem("sub_proj"), w.pre.o)
                stats("proj", XR, w.pre.b)
                aggregate("proj", w.pre.o)
            if w.post is not None:
                a = w.post
                dve.wait_ge(sem("wo_mm"), a.o + 1)
                dve.wait_ge(sem("bo_add"), a.o + 1)
                dve.tensor_tensor(x_of(XR, a.b), ma_ps[:, 0:2 * P], x_of(XR, a.b), ALU.add).then_inc(sem("attn_out"), 1)
                dve.wait_ge(sem("attn_out"), a.o + 1)
                if due(a.o):
                    dve.wait_ge(sem("sub_post"), a.o)
                stats("post", XR, a.b)
                aggregate("post", a.o)

        run_steps(dve, step)
        vector_tail(dve)

    @block.scalar
    def _(act):
        def step(w, _):
            for j in range(H):
                if w.cur is not None:
                    k = w.cur
                    act.wait_ge(sem("st_mm"), 16 * k.o + j + 1)
                    if due(4 * k.o + j // 4 - 1):
                        act.wait_ge(sem("pv_mm"), 4 * k.o + j // 4 - 1)
                    act.activation(probs[:, j % 8, :], st_ps[j % 2][:, :, :].rearrange("p a b -> p (a b)"),
                                   ACT.Exp, scale=SCALE).then_inc(sem("exp"), 1)
                if j == 1 and w.post is not None:
                    a = w.post
                    act.wait_ge(sem("pv_mm"), 4 * a.o + 4)
                    if due(a.o):
                        act.wait_ge(sem("yt_mm"), a.o)
                    act.activation(yraw[:, :], pv_ps[:, :], ACT.Copy).then_inc(sem("yraw"), 1)
                if j == 1 and w.next is not None:
                    c = w.next
                    act.wait_ge(sem("v_mm"), c.o + 1)
                    if due(4 * (c.o - 1)):
                        act.wait_ge(sem("pv_mm"), 4 * (c.o - 1))
                    act.wait_ge(sem("v_ones"), 4)
                    for u in range(2):
                        dst = vpad[c.p][:, :, :, :].rearrange("p t (n u) c -> p t n u c", u=2)[:, :, :, u, 8 * u:8 * u + HD]
                        src = ma_ps[:, 0:2 * P].rearrange("p (t n u d) -> p t n u d", t=2, u=2, d=HD)[:, :, :, u, :]
                        last = act.activation(dst, src, ACT.Copy)
                    last.then_inc(sem("v_in"), 1)
                if j == 2 and w.proj is not None:
                    c = w.proj
                    act.wait_ge(sem("hn_mm"), c.o + 1)
                    if due(c.o):
                        act.wait_ge(sem("v_mm"), c.o)
                    act.activation(hT[:, :], mb_ps[:, 0:T], ACT.Identity, scale=cols[:, 0, c.l:c.l + 1],
                                   bias=cols[:, 1, c.l:c.l + 1]).then_inc(sem("hT"), 1)
                if j == 4 and w.proj is not None:
                    c = w.proj
                    act.wait_ge(sem("qk_mm"), c.o + 1)
                    if due(c.o):
                        act.wait_ge(sem("rest"), c.o)
                    if due(16 * c.o):
                        act.wait_ge(sem("parts_out"), 16 * c.o)
                    for side in range(2):
                        half = slice(side * T, (side + 1) * T)
                        bias = cols[:, 2 + side, c.l:c.l + 1]
                        act.activation(qk32[:, half], mb_ps[:, half], ACT.Identity, bias=bias)
                        last = act.activation(parts[:, 0, half], mb_ps[:, half], ACT.Identity, bias=bias)
                    last.then_inc(sem("qk32"), 1)
                if j == 6 and w.last is not None:
                    a = w.last
                    act.wait_ge(sem("hn2_mm"), a.o + 1)
                    if due(2 * a.o):
                        act.wait_ge(sem("u_mm"), 2 * a.o)
                    act.activation(h2T[:, :], mb_ps[:, 0:T], ACT.Identity, scale=cols[:, 4, a.l:a.l + 1],
                                   bias=cols[:, 5, a.l:a.l + 1]).then_inc(sem("h2T"), 1)
                if j == 8 and w.last is not None:
                    a = w.last
                    if due(a.o):
                        act.wait_ge(sem("w2_mm"), a.o)
                    for c in range(NCH):
                        act.wait_ge(sem("u_mm"), 2 * a.o + 1 + c // 2)
                        src = (ma_ps, mb_ps)[c // 2]
                        act.activation(gel[:, c, :], src[:, (c % 2) * T:(c % 2 + 1) * T], ACT.Gelu,
                                       bias=cols[:, 7 + c, a.l:a.l + 1]).then_inc(sem("gelu"), 1)
                if j == 13 and w.post is not None:
                    a = w.post
                    act.wait_ge(sem("ynt_mm"), a.o + 1)
                    if due(a.o):
                        act.wait_ge(sem("wo_mm"), a.o)
                    act.activation(yT[:, :], mb_ps[:, 0:T], ACT.Copy).then_inc(sem("yT"), 1)

        act.wait_ge(sem("setup_in"), 16 * N_LOADS)
        run_steps(act, step)
        scalar_tail(act)

    @block.tensor
    def _(pe):
        pe.wait_ge(sem("setup_in"), 16 * N_LOADS)
        pe.wait_ge(sem("dve_const"), 3)
        pe.wait_ge(sem("bv_wide"), L)
        for l in range(L):
            pe.matmul(ma_ps[:, l * P:(l + 1) * P], yraw[:, l * P:(l + 1) * P], w_in[:, 4 * l + 3, :],
                      start=True, stop=True).then_inc(sem("bo_mm"), 1)
            pe.matmul(mb_ps[:, l * P:(l + 1) * P], consts["perm"][:, :], w_in[:, 4 * l + 3, :],
                      start=True, stop=True).then_inc(sem("wo_order_mm"), 1)
        pe.wait_ge(sem("setup_bo"), L)
        pe.wait_ge(sem("w_order"), 5 * L)

        def scores(bank, item, h, maxima, masked, transposed):
            rows = slice(0 if masked else ROW_PROD, ROWS if maxima else ROW_MAX)
            for a in range(2):
                b = a if masked else 1 - a
                x, y = (kst, qst) if transposed else (qst, kst)
                last = pe.matmul(bank[:, a, b * P:(b + 1) * P], x[item.p][rows, h, a * P:(a + 1) * P],
                                 y[item.p][rows, h, b * P:(b + 1) * P], start=True, stop=True)
            return last

        def weigh(item, q):
            pe.wait_ge(sem("exp"), 16 * item.o + 4 * q + 4)
            if q == 0:
                if due(item.o):
                    pe.wait_ge(sem("yraw"), item.o)
            s, u = q // 2, q % 2
            for t in range(2):
                for g in range(4):
                    h = 8 * s + 4 * u + g
                    last = pe.matmul(pv_ps[32 * g:32 * g + 32, s * T:(s + 1) * T],
                                     vpad[item.p][:, t, 8 * s + 2 * g + u, :],
                                     probs[:, h % 8, t * T:(t + 1) * T],
                                     start=(u == 0 and t == 0), stop=(u == 1 and t == 1),
                                     tile_position=(0, 32 * g), skip_group_check=True)
            last.then_inc(sem("pv_mm"), 1)

        def turn_maxima(item, g):
            c = 2 * item.o + g
            pe.wait_ge(sem("nm_parts"), c + 1)
            if due(c):
                pe.wait_ge(sem("nm_rows"), c)
            pe.transpose(mt_ps[:, g, 0:P], nm_parts[:, g, :, :].rearrange("p a b -> p (a b)"),
                         identb[:, :]).then_inc(sem("nm_mm"), 1)

        def row_scores(k, h):
            if h % 8 == 0:
                if due(96 * (k.o + 1)):
                    pe.wait_ge(sem(f"stack_in{h // 8}"), 96 * (k.o + 1))
            if due(16 * k.o + h - 1):
                pe.wait_ge(sem("maxed"), 16 * k.o + h - 1)
            scores(sm_ps[h % 2], k, h, False, True, False)
            scores(sm_ps[h % 2], k, h, False, False, False).then_inc(sem("sm_mm"), 1)

        def step(w, _):
            for j in range(H):
                if w.cur is not None:
                    k = w.cur
                    if j % 8 == 0:
                        if due(96 * (k.o + 1)):
                            pe.wait_ge(sem(f"stack_in{j // 8}"), 96 * (k.o + 1))
                        if due(16 * (k.o + 1)):
                            pe.wait_ge(sem(f"max_in{j // 8}"), 16 * (k.o + 1))
                    if j == 0:
                        pe.wait_ge(sem("v_in"), k.o + 1)
                    if due(16 * k.o + j - 1):
                        pe.wait_ge(sem("exp"), 16 * k.o + j - 1)
                    scores(st_ps[j % 2], k, j, True, True, True)
                if w.next is not None and j <= 10:
                    row_scores(w.next, j)
                if w.cur is not None:
                    scores(st_ps[j % 2], w.cur, j, True, False, True).then_inc(sem("st_mm"), 1)
                if w.next is not None and j in (10, 11, 12):
                    for h in {10: (11, 12, 13), 11: (14,), 12: (15,)}[j]:
                        row_scores(w.next, h)
                if j == 1 and w.post is not None:
                    weigh(w.post, 3)
                if j == 1 and w.next is not None:
                    c = w.next
                    if w.last is not None:
                        pe.wait_ge(sem("attn_out"), w.last.o + 1)
                    else:
                        if due(c.o):
                            pe.wait_ge(sem("v_in"), c.o)
                        if w.old is not None:
                            pe.wait_ge(sem("ffn_out"), w.old.o + 1)
                    for t in range(2):
                        last = pe.matmul(ma_ps[:, t * P:(t + 1) * P], hT[:, t * P:(t + 1) * P], wv[c.l][:, :],
                                         start=True, stop=True)
                    last.then_inc(sem("v_mm"), 1)
                if j == 2 and w.cur is not None:
                    turn_maxima(w.cur, 1)
                if j == 2 and w.proj is not None:
                    c = w.proj
                    if due(c.o):
                        pe.wait_ge(sem("qk32"), c.o)
                    pe.wait_ge(sem("hn"), c.o + 1)
                    for t in range(2):
                        last = pe.transpose(mb_ps[:, t * P:(t + 1) * P], hn[:, t, :], ident[:, :])
                    last.then_inc(sem("hn_mm"), 1)
                if j == 3 and w.post is not None:
                    a = w.post
                    if w.next is not None:
                        pe.wait_ge(sem("v_in"), w.next.o + 1)
                    elif w.last is not None:
                        pe.wait_ge(sem("attn_out"), w.last.o + 1)
                    elif w.old is not None:
                        pe.wait_ge(sem("ffn_out"), w.old.o + 1)
                    pe.wait_ge(sem("yraw"), a.o + 1)
                    for n in range(4):
                        m = 2 * (n % 2) + n // 2
                        last = pe.transpose(ma_ps[:, m * P:(m + 1) * P], yraw[:, n * P:(n + 1) * P], ident[:, :])
                    last.then_inc(sem("yt_mm"), 1)
                if j == 4 and w.proj is not None:
                    c = w.proj
                    pe.wait_ge(sem("hT"), c.o + 1)
                    for side, wt in enumerate((wq, wk)):
                        last = pe.matmul(mb_ps[:, side * T:(side + 1) * T], wt[c.l][:, :], hT[:, :], start=True, stop=True)
                    last.then_inc(sem("qk_mm"), 1)
                if j == 5 and w.cur is not None:
                    weigh(w.cur, 0)
                if j == 6 and w.last is not None:
                    a = w.last
                    if w.proj is not None:
                        pe.wait_ge(sem("qk32"), w.proj.o + 1)
                    pe.wait_ge(sem("hn2"), a.o + 1)
                    for t in range(2):
                        last = pe.transpose(mb_ps[:, t * P:(t + 1) * P], hn2[:, t, :], ident[:, :])
                    last.then_inc(sem("hn2_mm"), 1)
                if j == 8 and w.last is not None:
                    a = w.last
                    if w.post is not None:
                        pe.wait_ge(sem("yn"), w.post.o + 1)
                    elif w.next is not None:
                        pe.wait_ge(sem("v_in"), w.next.o + 1)
                    else:
                        pe.wait_ge(sem("attn_out"), a.o + 1)
                    pe.wait_ge(sem("h2T"), a.o + 1)
                    for m, bank in enumerate((ma_ps, mb_ps)):
                        for c in range(2):
                            last = pe.matmul(bank[:, c * T:(c + 1) * T], w1[a.l][:, (2 * m + c) * P:(2 * m + c + 1) * P],
                                             h2T[:, :], start=True, stop=True)
                        last.then_inc(sem("u_mm"), 1)
                if j == 9 and w.cur is not None:
                    weigh(w.cur, 1)
                if j == 9 and w.next is not None:
                    turn_maxima(w.next, 0)
                if j == 12 and w.last is not None:
                    e = w.last
                    pe.wait_ge(sem("gelu"), 4 * e.o + 4)
                    for t in range(2):
                        for c in range(NCH):
                            last = pe.matmul(ma_ps[:, t * P:(t + 1) * P], gel[:, c, t * P:(t + 1) * P],
                                             w2[e.l][:, c, :], start=(c == 0), stop=(c == NCH - 1))
                    last.then_inc(sem("w2_mm"), 1)
                if j == 13 and w.cur is not None:
                    weigh(w.cur, 2)
                if j == 13 and w.post is not None:
                    a = w.post
                    if w.last is None:
                        if w.proj is not None:
                            pe.wait_ge(sem("qk32"), w.proj.o + 1)
                        elif w.next is not None:
                            pe.wait_ge(sem("qk32"), w.next.o + 1)
                    pe.wait_ge(sem("yn"), a.o + 1)
                    yv = yn[:, :, :].rearrange("p (t m) d -> p t (m d)", t=2)
                    for t in range(2):
                        last = pe.transpose(mb_ps[:, t * P:(t + 1) * P], yv[:, t, :], ident[:, :])
                    last.then_inc(sem("ynt_mm"), 1)
                if j == 15 and w.post is not None:
                    a = w.post
                    if w.last is not None:
                        pe.wait_ge(sem("ffn_out"), w.last.o + 1)
                    pe.wait_ge(sem("yT"), a.o + 1)
                    for t in range(2):
                        last = pe.matmul(ma_ps[:, t * P:(t + 1) * P], yT[:, t * P:(t + 1) * P], wo[a.l][:, :],
                                         start=True, stop=True)
                    last.then_inc(sem("wo_mm"), 1)

        run_steps(pe, step)
        tensor_tail(pe)


_INS = ["L0_attn_" + n for n in ("x", "ln1_g", "ln1_b", "wq", "bq", "wk", "bk", "wv", "bv", "wo", "bo", "ln2_g", "ln2_b",
                                 "w1", "b1", "w2", "b2", "lnf_g", "lnf_b")]
_INS += ["L0_ffn_w_" + n for n in ("router", "gate", "up", "down")]


def kernel(**inputs):
    import concourse.bacc as _bacc
    from concourse.bass_utils import run_bass_kernel_spmd as _run

    nc = _bacc.Bacc("TRN2", target_bir_lowering=False, num_devices=1)
    arrays, aps = {}, {}
    given = {name: np.ascontiguousarray(inputs[name]) for name in _INS}
    given.update({"const_" + k: v for k, v in constants().items()})
    for name, a in given.items():
        arrays[f"in_{name}"] = a
        aps[name] = nc.dram_tensor(f"in_{name}", a.shape, mybir.dt.from_np(a.dtype), kind="ExternalInput").ap()
    out = nc.dram_tensor("out_0", (NB, T, P), F32, kind="ExternalOutput").ap()
    build(nc, aps, out)
    r = _run(nc, [arrays], core_ids=[0])
    return r.results[0]["out_0"]
```

```python
from contextlib import ExitStack

import numpy as np
import concourse.bass as bass
from concourse import mybir

F32 = mybir.dt.float32
BF16 = mybir.dt.bfloat16
U32 = mybir.dt.uint32
ALU = mybir.AluOpType
ACT = mybir.ActivationFunctionType
AX = mybir.AxisListType

P = 128
NB, T = 16, 256
H, HD = 16, 8
L = 2
FF = 512
NCH = FF // P
E, CAP = 32, 160
NT = NB * T // P
HALF = CAP // 2
EPS = 1e-5
SCALE = float(np.float32(1.0) / np.sqrt(HD).astype(np.float32))
BIG = -1e38

ROW_MASK = 0
N_MASK = 43
ROW_PROD = 64
ROW_ALL = 112
ROW_MAX = 113
ROWS = 116

DUMP = E * CAP
FIRST_LOOP, LAST_LOOP = 4, 11


def constants():
    q = np.arange(T)
    qrows = np.zeros((P, T), np.float32)
    krows = np.zeros((P, T), np.float32)
    for j in range(N_MASK):
        qrows[ROW_MASK + j, [3 * j, P + 1 + 3 * j]] = 1.0
        krows[ROW_MASK + j] = np.where(q < P, np.where(q > 3 * j, BIG, 0.0), np.where(q > P + 1 + 3 * j, BIG, 0.0))
    qrows[ROW_ALL] = (q % 3 == 0) & (q < P)
    krows[ROW_ALL] = np.where(q >= P, BIG, 0.0)
    krows[ROW_MAX:ROW_MAX + 3] = 1.0
    ident = np.eye(P, dtype=np.float32)
    tri = np.triu(np.ones((P, P), np.float32))
    rev = np.tile(E - np.arange(E, dtype=np.float32), (P, 1))
    order = np.arange(P).reshape(2, 2, 4, HD).transpose(0, 2, 1, 3).reshape(-1)
    perm = np.eye(P, dtype=np.float32)[:, order]
    dump = DUMP + np.arange(NT, dtype=np.float32)[None, :] * P + np.arange(P, dtype=np.float32)[:, None]
    return {"qrows": qrows, "krows": krows, "ident": ident, "tri": tri, "rev": rev, "dump": dump, "perm": perm}


class Item:

    def __init__(self, n, b, layer, parity):
        self.o, self.b, self.l, self.p = n, b, layer, parity


AHEAD = 5


def item_at(n):
    if n < 0 or n >= 2 * NB:
        return None
    for b in range(NB):
        if n == max(b, 2 * b - AHEAD + 1):
            return Item(n, b, 0, n % 2)
        if n == min(2 * b + AHEAD, NB + b):
            return Item(n, b, 1, n % 2)


class Step:

    def __init__(self, s=None, i=None, c=0):
        def at(d):
            if i is None:
                return item_at(s + d)
            k = c + d
            b = i + (k + AHEAD - 1) // 2 if k % 2 == 0 else i + (k - AHEAD) // 2
            return Item(2 * i + k, b, k % 2, k % 2)
        self.pre = at(3)
        self.raw = self.pre if self.pre is not None and self.pre.l == 0 else None
        self.proj = at(2)
        self.next = at(1)
        self.cur = at(0)
        self.post = at(-1)
        self.last = at(-2)
        self.old = at(-3)
        old, oldest = self.old, at(-4)
        self.final = old if old is not None and old.l == 1 else None
        self.router = oldest if oldest is not None and oldest.l == 1 else None


def build(nc, ins, out):
    ctx = ExitStack()
    with ctx:
        _build(nc, ctx, ins, out)


def _build(nc, ctx, ins, out):
    def sb(name, shape, dt=F32):
        return ctx.enter_context(nc.sbuf_tensor(name, shape, dt))

    def ps(name, shape, dt=F32):
        return ctx.enter_context(nc.psum_tensor(name, shape, dt))

    sems = {}

    def sem(name):
        if name not in sems:
            sems[name] = ctx.enter_context(nc.semaphore(name))
        return sems[name]

    def due(value):
        return not isinstance(value, int) or value > 0

    n_holds = [0]

    def hold(eng, value):
        if value is not None and not isinstance(value, int):
            n_holds[0] += 1
            to = scratch[:, n_holds[0]:n_holds[0] + 1]
            if eng is nc.vector:
                eng.tensor_copy(to, scratch[:, 0:1])
            else:
                eng.tensor_tensor(to, scratch[:, 0:1], scratch[:, 0:1], ALU.add)

    parts_d = [nc.dram_tensor(f"parts_d{p}", (3, 2, HD, H, T), BF16, kind="Internal").ap() for p in range(2)]
    xbuf_d = nc.dram_tensor("xbuf_d", (DUMP + NB * T, P), F32, kind="Internal").ap()
    ybuf_d = nc.dram_tensor("ybuf_d", (DUMP + P, P), F32, kind="Internal").ap()

    XO = sb("x_outer", [P, NT * P])
    XR = sb("x_inner", [P, NT * P])
    qst = [sb(f"q_stack{p}", [P, H, T], BF16) for p in range(2)]
    kst = [sb(f"k_stack{p}", [P, H, T], BF16) for p in range(2)]
    vpad = [sb(f"v_pad{p}", [P, 2, H, 32]) for p in range(2)]
    probs = sb("probs", [P, 8, 2 * T])
    hn = sb("hn", [P, 2, P])
    hT = sb("hT", [P, T])
    qk32 = sb("qk32", [P, 2 * T])
    rest = sb("rest", [P, 2 * T])
    parts = sb("parts", [P, 3, 2 * T], BF16)
    maxes = [sb(f"maxes{p}", [P, H, 2]) for p in range(2)]
    nm_rest = sb("nm_rest", [P, 2, 16])
    nm_parts = sb("nm_parts", [P, 2, 8, 16], BF16)
    nm_rows = sb("nm_rows", [48, 2, P], BF16)
    yraw = sb("yraw", [P, 2 * T])
    rden = sb("rden", [P, 2 * H])
    yn = sb("yn", [P, 2 * H, HD])
    yT = sb("yT", [P, T])
    hn2 = sb("hn2", [P, 2, P])
    h2T = sb("h2T", [P, T])
    gel = sb("gel", [P, NCH, T])
    w_in = gel[:, :, :].rearrange("p k t -> p (k t)").rearrange("p (n c) -> p n c", c=P)
    fin = sb("fin", [P, 2, P])
    bn = {k: sb(f"bn_{k}", [P, 2, 6]) for k in ("raw", "proj", "post", "f1", "f2", "f3")}
    mv = {k: sb(f"mv_{k}", [P, 2, 2]) for k in bn}
    rs = {k: sb(f"rs_{k}", [P, 2, 2]) for k in bn}
    consts = {k: sb(f"c_{k}", [P, v.shape[1]]) for k, v in constants().items()}
    ident = consts["ident"]
    identb = sb("identb", [P, P], BF16)
    trib = sb("trib", [P, P], BF16)
    onesb = sb("onesb", [P, P], BF16)
    eps_mh = sb("eps_mh", [P, 2, 2])
    wq = [sb(f"wq{l}", [P, P]) for l in range(L)]
    wk = [sb(f"wk{l}", [P, P]) for l in range(L)]
    wv = [sb(f"wv{l}", [P, P]) for l in range(L)]
    wo = [sb(f"wo{l}", [P, P]) for l in range(L)]
    w1 = [sb(f"w1{l}", [P, FF]) for l in range(L)]
    w2 = [sb(f"w2{l}", [P, NCH, P]) for l in range(L)]
    cols = sb("cols", [P, 7 + NCH, L])
    bo_row = [sb(f"bo_row{l}", [P, 2, P]) for l in range(L)]
    b2_row = [sb(f"b2_row{l}", [P, 2, P]) for l in range(L)]
    lnf = sb("lnf", [P, 2, P])
    wr = sb("wr", [P, E])
    zero = sb("zero", [P, 512])
    scratch = sb("scratch", [P, 64])

    wgate = sb("wgate", [P, E, P])
    wup = sb("wup", [P, E, P])
    wdown = sb("wdown", [P, E, P])
    logits = sb("logits", [P, NT * E])
    slot_in = sb("slot_in", [P, NT], U32)
    slot_out = sb("slot_out", [P, NT], U32)
    small = {k: sb(f"r_{k}", [P, NT]) for k in ("top", "rev", "sum", "gate", "place", "taken", "slot", "to")}
    bn_out = sb("bn_out", [P, NT, 6])
    mv_out = sb("mv_out", [P, NT, 2])
    rs_out = sb("rs_out", [P, NT, 2])
    shift = sb("shift", [P, NT])
    HALF_NE = NT // 2 * E
    diff = probs[:, 4:6, :].rearrange("p a b -> p (a b)")
    expd = probs[:, 6:8, :].rearrange("p a b -> p (a b)")
    yg = probs[:, :, :].rearrange("p a (b c) -> p (a b) c", c=P)
    cand = gel[:, :, :].rearrange("p a b -> p (a b)")
    onehot = parts[:, 0:2, :].rearrange("p a b -> p (a b)")
    xeT = yraw[:, :].rearrange("p (a b) -> p a b", a=2)[:, :, 0:CAP]
    sg = qk32[:, :].rearrange("p (a b) -> p a b", a=2)[:, :, 0:CAP]
    hid = rest[:, :].rearrange("p (a b) -> p a b", a=2)[:, :, 0:CAP]
    yout = vpad[0][0:HALF, :, :, :].rearrange("p t h c -> p (t h c)").rearrange("p (m n c) -> p m n c", m=4, n=2)

    st_ps = [ps(f"st_ps{i}", [P, 2, T]) for i in range(2)]
    sm_ps = [ps(f"sm_ps{i}", [P, 2, T]) for i in range(2)]
    pv_ps = ps("pv_ps", [P, 2 * T])
    mt_ps = ps("mt_ps", [P, 2, 512], BF16)
    ma_ps = ps("ma_ps", [P, 512])
    mb_ps = ps("mb_ps", [P, 512])

    block = ctx.enter_context(nc.Block())

    def x_of(buf, b):
        if isinstance(b, int):
            return buf[:, b * 2 * P:(b + 1) * 2 * P]
        return buf[:, bass.ds(b * (2 * P), 2 * P)]

    def tiles(ap):
        return ap.rearrange("p (t c) -> p t c", t=2)

    def tile_of(buf, b, t):
        if isinstance(b, int):
            return buf[:, (2 * b + t) * P:(2 * b + t + 1) * P]
        return buf[:, bass.ds(b * (2 * P) + t * P, P)]

    def run_steps(eng, step, first=-3):
        for s in range(first, 2 * FIRST_LOOP):
            step(Step(s), None)
        with eng.Fori(FIRST_LOOP, LAST_LOOP + 1) as i:
            for c in range(2):
                step(Step(i=i, c=c), (i, c))
        for s in range(2 * LAST_LOOP + 2, 2 * NB + 4):
            step(Step(s), None)

    N_LOADS = len(consts) + L * (6 + 2 + 1 + 4) + 5 + 3


    def xt_tile(n):
        return XR[:, n * P:(n + 1) * P]

    def expert_rows(q):
        buf = (qst[0], qst[1], kst[0], kst[1])[q]
        return buf[0:HALF, :, :].rearrange("p h t -> p (h t)").bitcast(F32).rearrange("p (n c) -> p n c", c=P)

    def sync_tail(sp):
        sp.wait_ge(sem("scattered"), 16 * NT)
        for q in range(4):
            rows = xbuf_d[q * 8 * CAP:(q + 1) * 8 * CAP, :].rearrange("(n p) c -> p n c", p=HALF)
            sp.dma_start(expert_rows(q), rows).then_inc(sem(f"buf_in{q}"), 16)
        for e in range(E):
            sp.wait_ge(sem("y_out"), e + 1)
            rows = ybuf_d[e * CAP:(e + 1) * CAP, :].rearrange("(n p) c -> p n c", p=HALF)
            sp.dma_start(rows, yout[:, e % 4, :, :]).then_inc(sem(f"y_stored{e % 4}"), 16)
        ov = out.rearrange("b (t p) c -> p (b t) c", p=P)
        for g in range(NT // 4):
            sp.wait_ge(sem("result"), g + 1)
            sp.dma_start(ov[:, 4 * g:4 * g + 4, :], XO[:, g * 4 * P:(g + 1) * 4 * P].rearrange("p (n c) -> p n c", c=P)
                         ).then_inc(sem("stored"), 16)
        sp.wait_ge(sem("stored"), 16 * (NT // 4))

    def pool_tail(pool):
        pool.wait_ge(sem("dram_zero"), 16 * (DUMP // (4 * P) + 1))
        pool.wait_ge(sem("xt"), NB)
        for n in range(NT):
            pool.wait_ge(sem("slots"), n // (NT // 2) + 1)
            pool.indirect_dma_start(xbuf_d, bass.IndirectOffsetOnAxis(ap=slot_in[:, n:n + 1], axis=0),
                                    xt_tile(n), None).then_inc(sem("scattered"), 16)
        for m in range(4):
            pool.wait_ge(sem(f"y_stored{m}"), 16 * (E // 4))
        for n in range(NT):
            pool.indirect_dma_start(yg[:, n, :], None, ybuf_d,
                                    bass.IndirectOffsetOnAxis(ap=slot_out[:, n:n + 1], axis=0)).then_inc(sem(f"y_in{n // 4}"), 16)

    def scalar_tail(act):
        for g in range(NT // 4):
            if g == NT // 4 - 2:
                act.wait_ge(sem("lg_diff"), 1)
                act.activation(expd[:, 0:HALF_NE], diff[:, 0:HALF_NE], ACT.Exp).then_inc(sem("expd"), 1)
            act.wait_ge(sem("rt_mm"), g + 1)
            if due(g - 3):
                act.wait_ge(sem("lg_mm"), g - 3)
            act.activation(probs[:, g % 4, :], (ma_ps, mb_ps)[g % 2][:, :], ACT.Copy).then_inc(sem("rt_in"), 1)
        act.wait_ge(sem("lg_diff"), 2)
        act.activation(expd[:, HALF_NE:], diff[:, HALF_NE:], ACT.Exp).then_inc(sem("expd"), 1)
        for e in range(E):
            act.wait_ge(sem("et_mm"), e + 1)
            if due(e - 1):
                act.wait_ge(sem("gu_mm"), e - 1)
            act.activation(xeT[:, e % 2, :], st_ps[e % 2][:, 0, 0:CAP], ACT.Copy).then_inc(sem("xeT"), 1)
            act.wait_ge(sem("gu_mm"), e + 1)
            if due(e - 1):
                act.wait_ge(sem("act"), e - 1)
            act.activation(sg[:, e % 2, :], sm_ps[e % 2][:, 0, 0:CAP], ACT.Silu).then_inc(sem("silu"), 1)
        for g in range(NT // 4 + 1):
            if g < NT // 4:
                s = slice(4 * g, 4 * g + 4)
                act.wait_ge(sem("mv_out"), 4 * g + 4)
                act.activation(rs_out[:, s, 0], mv_out[:, s, 1], ACT.Sqrt, bias=eps_mh[:, 0, 0:1]).then_inc(sem("std_out"), 1)
            if g >= 1:
                act.wait_ge(sem("shift"), g)
                for n in range(4 * g - 4, 4 * g):
                    last = act.activation(xt_tile(n), xt_tile(n), ACT.Identity, scale=rs_out[:, n, 1:2], bias=shift[:, n:n + 1])
                last.then_inc(sem("normed"), 1)

    def vector_tail(dve):
        n_link = [0]

        def link(ins):
            n_link[0] += 1
            ins.then_inc(sem("route"), 1)
            dve.wait_ge(sem("route"), n_link[0])

        def route_half(m):
            n_tiles = NT // 2
            flat = slice(m * HALF_NE, (m + 1) * HALF_NE)
            ts = slice(m * n_tiles, (m + 1) * n_tiles)

            def by_tile(buf):
                return buf[:, flat].rearrange("p (n e) -> p n e", e=E)

            def wide(ap):
                return ap.rearrange("p (n o) -> p n o", o=1).to_broadcast([P, n_tiles, E])

            r = {k: v[:, ts] for k, v in small.items()}
            lg, cd = by_tile(logits), by_tile(cand)
            dve.wait_ge(sem("lg_mm"), 4 * m + 4)
            link(dve.tensor_copy(logits[:, flat], st_ps[m][:, :, :].rearrange("p a b -> p (a b)")))
            link(dve.tensor_reduce(r["top"], lg, AX.X, ALU.max))
            dve.tensor_tensor(by_tile(diff), lg, wide(r["top"]), ALU.subtract).then_inc(sem("lg_diff"), 1)
            dve.wait_ge(sem("lg_diff"), m + 1)
            link(dve.scalar_tensor_tensor(out=cd, in0=by_tile(diff), scalar=0.0,
                                          in1=consts["rev"][:, :].rearrange("p (o e) -> p o e", o=1).to_broadcast([P, n_tiles, E]),
                                          op0=ALU.is_ge, op1=ALU.mult))
            link(dve.tensor_reduce(r["rev"], cd, AX.X, ALU.max))
            dve.tensor_tensor(by_tile(onehot), cd, wide(r["rev"]), ALU.is_equal).then_inc(sem("onehot"), 1)
            dve.wait_ge(sem("expd"), m + 1)
            link(dve.tensor_reduce(r["sum"], by_tile(expd), AX.X, ALU.add))
            link(dve.reciprocal(r["gate"], r["sum"]))
            dve.wait_ge(sem("tot_mm"), m + 1)
            link(dve.tensor_copy(diff[:, flat], (pv_ps, ma_ps)[m][:, :]))
            carry = diff[:, HALF_NE - E:HALF_NE]
            if m == 1:
                link(dve.tensor_tensor(diff[:, HALF_NE:HALF_NE + E], diff[:, HALF_NE:HALF_NE + E], carry, ALU.add))
            a, b, d = diff[:, flat], expd[:, flat], 1
            while d < n_tiles:
                dve.tensor_tensor(b[:, d * E:], a[:, d * E:], a[:, 0:(n_tiles - d) * E], ALU.add).then_inc(sem("route"), 1)
                dve.tensor_copy(b[:, 0:d * E], a[:, 0:d * E]).then_inc(sem("route"), 1)
                n_link[0] += 2
                dve.wait_ge(sem("route"), n_link[0])
                a, b, d = b, a, 2 * d
            dve.wait_ge(sem("inc_mm"), m + 1)
            src = sm_ps[m][:, :, :].rearrange("p a b -> p (a b)")
            lo = m * HALF_NE
            if m == 0:
                dve.tensor_copy(logits[:, 0:E], src[:, 0:E]).then_inc(sem("route"), 1)
            else:
                dve.tensor_tensor(logits[:, lo:lo + E], src[:, 0:E], carry, ALU.add).then_inc(sem("route"), 1)
            dve.tensor_tensor(logits[:, lo + E:lo + HALF_NE], src[:, E:], a[:, 0:HALF_NE - E], ALU.add).then_inc(sem("route"), 1)
            n_link[0] += 2
            dve.wait_ge(sem("route"), n_link[0])
            link(dve.tensor_tensor(logits[:, flat], logits[:, flat], onehot[:, flat], ALU.mult))
            link(dve.tensor_reduce(r["place"], lg, AX.X, ALU.add))
            link(dve.tensor_single_scalar(r["taken"], r["place"], float(CAP), ALU.is_le))
            link(dve.scalar_tensor_tensor(out=r["slot"], in0=r["rev"], scalar=-float(CAP), in1=r["place"],
                                          op0=ALU.mult, op1=ALU.add))
            link(dve.tensor_scalar(r["slot"], r["slot"], float(E * CAP - 1), None, ALU.add))
            link(dve.tensor_tensor(r["to"], r["slot"], consts["dump"][:, ts], ALU.subtract))
            link(dve.tensor_tensor(r["to"], r["to"], r["taken"], ALU.mult))
            link(dve.tensor_tensor(slot_in[:, ts], r["to"], consts["dump"][:, ts], ALU.add))
            link(dve.tensor_scalar(r["slot"], r["slot"], -float(DUMP), None, ALU.add))
            link(dve.tensor_tensor(r["slot"], r["slot"], r["taken"], ALU.mult))
            dve.tensor_scalar(slot_out[:, ts], r["slot"], float(DUMP), None, ALU.add).then_inc(sem("slots"), 1)

        for m in range(2):
            route_half(m)
        for e in range(E):
            dve.wait_ge(sem("silu"), e + 1)
            if due(e - 1):
                dve.wait_ge(sem("ye_mm"), e - 1)
            dve.tensor_tensor(hid[:, e % 2, :], sm_ps[e % 2][:, 1, 0:CAP], sg[:, e % 2, :], ALU.mult).then_inc(sem("act"), 1)
            if e >= 1:
                take_y(dve, e - 1)
        take_y(dve, E - 1)
        for g in range(NT // 4):
            for n in range(4 * g, 4 * g + 4):
                dve.wait_ge(sem(f"y_in{g}"), 64)
                dve.scalar_tensor_tensor(out=xt_tile(n), in0=yg[:, n, :], scalar=small["gate"][:, n:n + 1], in1=xt_tile(n),
                                         op0=ALU.mult, op1=ALU.add).then_inc(sem("z"), 1)
            for n in range(4 * g, 4 * g + 4):
                dve.wait_ge(sem("z"), n + 1)
                dve.bn_stats(bn_out[:, n, :], xt_tile(n)).then_inc(sem("bn_out"), 1)
            for n in range(4 * g, 4 * g + 4):
                dve.wait_ge(sem("bn_out"), n + 1)
                dve.bn_aggr(mv_out[:, n, :], bn_out[:, n, :]).then_inc(sem("mv_out"), 1)
            if g >= 1:
                minus_mean(dve, g - 1)
            if g >= 2:
                add_outer(dve, g - 2)
        minus_mean(dve, NT // 4 - 1)
        add_outer(dve, NT // 4 - 2)
        add_outer(dve, NT // 4 - 1)

    def minus_mean(dve, g):
        s = slice(4 * g, 4 * g + 4)
        dve.wait_ge(sem("std_out"), g + 1)
        dve.reciprocal(rs_out[:, s, 1], rs_out[:, s, 0]).then_inc(sem("rs_out"), 1)
        dve.wait_ge(sem("rs_out"), g + 1)
        dve.scalar_tensor_tensor(out=shift[:, s], in0=mv_out[:, s, 0], scalar=-1.0, in1=rs_out[:, s, 1],
                                 op0=ALU.mult, op1=ALU.mult).then_inc(sem("shift"), 1)

    def add_outer(dve, g):
        s = slice(g * 4 * P, (g + 1) * 4 * P)
        dve.wait_ge(sem("normed"), g + 1)
        dve.tensor_tensor(XO[:, s], XO[:, s], XR[:, s], ALU.add).then_inc(sem("result"), 1)

    def take_y(dve, e):
        dve.wait_ge(sem("ye_mm"), e + 1)
        if due(e // 4):
            dve.wait_ge(sem(f"y_stored{e % 4}"), 16 * (e // 4))
        dve.tensor_copy(yout[:, e % 4, :, :], (ma_ps, mb_ps)[e % 2][0:HALF, 0:2 * P].rearrange("p (n c) -> p n c", n=2)
                        ).then_inc(sem("y_out"), 1)

    def tensor_tail(pe):
        pe.wait_ge(sem("exp"), 16 * 2 * NB)
        pe.wait_ge(sem("maxed"), 16 * 2 * NB)
        pe.wait_ge(sem("ffn_out"), 2 * NB)

        def route(g):
            pe.wait_ge(sem("rt_in"), g + 1)
            for n in range(4 * g, 4 * g + 4):
                m = n % 16
                last = pe.matmul(st_ps[n // 16][:, m // 8, (m % 8) * E:(m % 8 + 1) * E], probs[:, g % 4, (n % 4) * P:(n % 4 + 1) * P],
                                 wr[:, :], start=True, stop=True)
            last.then_inc(sem("lg_mm"), 1)

        def count(m):
            flat = slice(m * HALF_NE, (m + 1) * HALF_NE)
            pe.wait_ge(sem("onehot"), m + 1)
            pe.matmul(sm_ps[m][:, :, :].rearrange("p a b -> p (a b)"), trib[:, :], onehot[:, flat],
                      start=True, stop=True).then_inc(sem("inc_mm"), 1)
            pe.matmul((pv_ps, ma_ps)[m][:, :], onesb[:, :], onehot[:, flat], start=True, stop=True).then_inc(sem("tot_mm"), 1)

        for g in range(NT // 4):
            if g == NT // 4 - 2:
                count(0)
            pe.wait_ge(sem("xt"), 2 * g + 2)
            if due(g - 1):
                pe.wait_ge(sem("rt_in"), g - 1)
            if g == 0:
                pe.wait_ge(sem("gelu"), 4 * 2 * NB)
            for n in range(4):
                last = pe.transpose((ma_ps, mb_ps)[g % 2][:, n * P:(n + 1) * P], xt_tile(4 * g + n), ident[:, :])
            last.then_inc(sem("rt_mm"), 1)
            if g >= 1:
                route(g - 1)
        route(NT // 4 - 1)
        count(1)
        pe.wait_ge(sem("experts_in"), 48)
        pe.wait_ge(sem("slots"), 2)

        def turn(e):
            if e % 8 == 0:
                pe.wait_ge(sem(f"buf_in{e // 8}"), 16)
            if due(e - 1):
                pe.wait_ge(sem("xeT"), e - 1)
            for a in range(2):
                last = pe.transpose(st_ps[e % 2][:, 0, a * HALF:(a + 1) * HALF], expert_rows(e // 8)[:, 2 * (e % 8) + a, :],
                                    ident[0:HALF, 0:HALF])
            last.then_inc(sem("et_mm"), 1)

        def down(e):
            pe.wait_ge(sem("act"), e + 1)
            if due(e - 1):
                pe.wait_ge(sem("y_out"), e - 1)
            for a in range(2):
                last = pe.matmul((ma_ps, mb_ps)[e % 2][0:HALF, a * P:(a + 1) * P], hid[:, e % 2, a * HALF:(a + 1) * HALF],
                                 wdown[:, e, :], start=True, stop=True)
            last.then_inc(sem("ye_mm"), 1)

        turn(0)
        for e in range(E):
            if e + 1 < E:
                turn(e + 1)
            pe.wait_ge(sem("xeT"), e + 1)
            if due(e - 1):
                pe.wait_ge(sem("act"), e - 1)
            for k, w in enumerate((wgate, wup)):
                last = pe.matmul(sm_ps[e % 2][:, k, 0:CAP], w[:, e, :], xeT[:, e % 2, :], start=True, stop=True)
            last.then_inc(sem("gu_mm"), 1)
            if e >= 1:
                down(e - 1)
        down(E - 1)

    @block.sync
    def _(sp):
        xv = ins["L0_attn_x"].rearrange("b (t p) c -> p (b t) c", p=P)
        xo = XO[:, :].rearrange("p (n c) -> p n c", c=P)
        sp.dma_start(xo[:, 0:2, :], xv[:, 0:2, :]).then_inc(sem("x_first"), 16)
        loads = []
        for k in consts:
            loads.append((consts[k][:, :], ins["const_" + k]))
        for n, name in ((0, "ln1_g"), (1, "ln1_b"), (4, "ln2_g"), (5, "ln2_b"), (6, "bv")):
            loads.append((cols[:, n, :].rearrange("p (l o) -> p l o", o=1), ins["L0_attn_" + name].rearrange("l (p o) -> p l o", o=1)))
        for l in range(L):
            row = lambda name: ins["L0_attn_" + name][l:l + 1, :].to_broadcast([P, P])
            for n, name in ((2, "bq"), (3, "bk")):
                loads.append((cols[:, n, l:l + 1], ins["L0_attn_" + name][l].rearrange("(h d o) -> d h o", h=H, o=1)))
            for n, name in enumerate(("wq", "wk", "wv", "wo")):
                loads.append((w_in[:, 4 * l + n, :], ins["L0_attn_" + name][l]))
            loads += [(w1[l][:, :], ins["L0_attn_w1"][l]),
                      (w2[l][:, :, :], ins["L0_attn_w2"][l].rearrange("(k p) n -> p k n", p=P)),
                      (cols[:, 7:7 + NCH, l:l + 1], ins["L0_attn_b1"][l].rearrange("(k p o) -> p k o", p=P, o=1))]
            for t in range(2):
                loads.append((bo_row[l][:, t, :], row("bo")))
                loads.append((b2_row[l][:, t, :], row("b2")))
        loads.append((lnf[:, 0, :], ins["L0_attn_lnf_g"].rearrange("(o c) -> o c", o=1).to_broadcast([P, P])))
        loads.append((lnf[:, 1, :], ins["L0_attn_lnf_b"].rearrange("(o c) -> o c", o=1).to_broadcast([P, P])))
        loads.append((wr[:, :], ins["L0_ffn_w_router"]))
        with nc.allow_non_contiguous_dma(reason="a vector goes to one element a partition"):
            for dst, src in loads:
                sp.dma_start(dst, src).then_inc(sem("setup_in"), 16)
        assert len(loads) == N_LOADS, len(loads)
        sp.dma_start(xo[:, 2:8, :], xv[:, 2:8, :]).then_inc(sem("x_rest"), 16)

        def read_stack(item, g):
            hs = slice(8 * g, 8 * g + 8)
            d = parts_d[item.p]
            sp.wait_ge(sem("stack_const"), 2)
            if g == 0:
                sp.wait_ge(sem("parts_out"), 16 * item.o + 16)
            if (g == 1 or isinstance(item.o, int)) and due(16 * item.o - 32 + 8 * g + 8):
                sp.wait_ge(sem("st_mm"), 16 * item.o - 32 + 8 * g + 8)
            for n, m, a in ((0, 3, 0), (3, 2, 1), (5, 1, 2)):
                rows = slice(ROW_PROD + 8 * n, ROW_PROD + 8 * (n + m))
                q = d[a, 0:1][:, :, hs, :].rearrange("n d h t -> n d (h t)")
                sp.dma_start(qst[item.p][rows, hs, :], q.to_broadcast([m, HD, 8 * T])).then_inc(sem(f"stack_in{g}"), 16)
                k = d[0:m, 1][:, :, hs, :].rearrange("n d h t -> n d (h t)")
                sp.dma_start(kst[item.p][rows, hs, :], k).then_inc(sem(f"stack_in{g}"), 16)

        def max_rows(item, g):
            sp.wait_ge(sem("nm_rows"), 2 * item.o + g + 1)
            sp.dma_start(qst[item.p][ROW_MAX:ROW_MAX + 3, 8 * g:8 * g + 8, :],
                         nm_rows[:, g, :]).then_inc(sem(f"max_in{g}"), 16)

        def step(w, _):
            if w.next is not None:
                read_stack(w.next, 1)
            if w.cur is not None:
                max_rows(w.cur, 1)
            if w.proj is not None:
                c = w.proj
                if isinstance(c.o, int):
                    if due(96 * (c.o - 1)):
                        sp.wait_ge(sem("stack_in1"), 96 * (c.o - 1))
                sp.wait_ge(sem("parts"), c.o + 1)
                sp.dma_start(parts_d[c.p].rearrange("a s d h t -> (d h) (a s) t"),
                             parts[:, :, :].rearrange("p a (s t) -> p (a s) t", s=2)).then_inc(sem("parts_out"), 16)
            if w.next is not None:
                max_rows(w.next, 0)
            if w.proj is not None:
                read_stack(w.proj, 0)

        step(Step(-3), None)
        step(Step(-2), None)
        sp.dma_start(xo[:, 8:, :], xv[:, 8:, :]).then_inc(sem("x_rest"), 16)
        for s in range(-1, 3):
            step(Step(s), None)
        sp.wait_ge(sem("zeroed"), 1)
        for n in range(DUMP // (P * 4)):
            sp.dma_start(xbuf_d[n * 4 * P:(n + 1) * 4 * P, :].rearrange("(p r) c -> p (r c)", p=P),
                         zero[:, :]).then_inc(sem("dram_zero"), 16)
        sp.dma_start(ybuf_d[DUMP:DUMP + P, :], zero[:, 0:P]).then_inc(sem("dram_zero"), 16)
        for n, (w, name) in enumerate(((wgate, "gate"), (wup, "up"), (wdown, "down"))):
            step(Step(3 + n), None)
            sp.dma_start(w[:, :, :], ins["L0_ffn_w_" + name].rearrange("e h f -> h e f")).then_inc(sem("experts_in"), 16)
        run_steps(sp, step, 6)
        sync_tail(sp)

    @block.gpsimd
    def _(pool):
        pool.memset(zero[:, :], 0.0).then_inc(sem("zeroed"), 1)
        pool.memset(eps_mh[:, :, 0:1], EPS).then_inc(sem("eps"), 1)
        pool.memset(eps_mh[:, :, 1:2], -0.5).then_inc(sem("eps"), 1)
        for p in range(2):
            pool.memset(vpad[p][:, :, :, :], 0.0).then_inc(sem("v_zero"), 1)
        pool.wait_ge(sem("v_zero"), 2)
        for p in range(2):
            for u in range(2):
                pool.memset(vpad[p][:, :, :, :].rearrange("p t (s u) c -> p (t s) u c", u=2)[:, :, u, 16 + u:17 + u],
                            1.0).then_inc(sem("v_ones"), 1)
        pool.wait_ge(sem("eps"), 2)
        pool.wait_ge(sem("scratch"), 1)

        def rstd(key, o, count):
            pool.wait_ge(sem(f"mv_{key}"), count)
            pool.tensor_tensor(rs[key][:, :, 0:1], mv[key][:, :, 1:2], eps_mh[:, :, 0:1], ALU.add).then_inc(sem(f"ve_{key}"), 1)
            pool.wait_ge(sem(f"ve_{key}"), o + 1)
            pool.tensor_tensor(rs[key][:, :, 1:2], rs[key][:, :, 0:1], eps_mh[:, :, 1:2], ALU.pow).then_inc(sem(f"rs_{key}"), 1)

        def normalize(key, o, count, dst, src, done):
            rstd(key, o, count)
            pool.tensor_tensor(dst, src, mv[key][:, :, 0:1].to_broadcast([P, 2, P]), ALU.subtract).then_inc(sem(f"sub_{key}"), 1)
            pool.wait_ge(sem(f"sub_{key}"), o + 1)
            pool.wait_ge(sem(f"rs_{key}"), o + 1)
            hold(pool, o)
            pool.tensor_tensor(dst, dst, rs[key][:, :, 1:2].to_broadcast([P, 2, P]), ALU.mult).then_inc(sem(done), 1)

        def step(w, _):
            if w.router is not None:
                f = w.router.b
                normalize("f3", f, 2 * f + 2, tiles(x_of(XR, f)), tiles(x_of(XO, f)), "xt")
            if w.final is not None:
                f = w.final.b
                normalize("f1", f, 2 * f + 2, fin[:, :, :], tiles(x_of(XR, f)), "f1_norm")
                pool.wait_ge(sem("f1_norm"), f + 1)
                pool.tensor_tensor(fin[:, :, :], fin[:, :, :], lnf[:, 0:1, :].to_broadcast([P, 2, P]), ALU.mult).then_inc(sem("f1_g"), 1)
                pool.wait_ge(sem("f1_g"), f + 1)
                pool.tensor_tensor(fin[:, :, :], fin[:, :, :], lnf[:, 1:2, :].to_broadcast([P, 2, P]), ALU.add).then_inc(sem("f1_b"), 1)
            if w.proj is not None:
                o = w.proj.o
                pool.wait_ge(sem("qk32"), o + 1)
                if due(o):
                    pool.wait_ge(sem("part1"), o)
                pool.tensor_tensor(rest[:, :], qk32[:, :], parts[:, 0, :], ALU.subtract).then_inc(sem("rest"), 1)
            if w.post is not None:
                a = w.post
                pool.wait_ge(sem("setup_bo"), L)
                pool.tensor_tensor(tiles(x_of(XR, a.b)), tiles(x_of(XR, a.b)), bo_row[a.l][:, :, :], ALU.add).then_inc(sem("bo_add"), 1)
            if w.proj is not None:
                pool.wait_ge(sem("part1"), w.proj.o + 1)
                pool.tensor_tensor(parts[:, 2, :], rest[:, :], parts[:, 1, :], ALU.subtract).then_inc(sem("parts"), 1)
            if w.final is not None:
                f = w.final.b
                normalize("f2", f, 2 * f + 2, fin[:, :, :], fin[:, :, :], "f2_norm")
                pool.wait_ge(sem("f2_norm"), f + 1)
                hold(pool, f)
                pool.tensor_tensor(tiles(x_of(XO, f)), tiles(x_of(XO, f)), fin[:, :, :], ALU.add).then_inc(sem("x_attn"), 1)
            if w.raw is not None:
                r = w.raw.b
                normalize("raw", r, 2 * r + 2, tiles(x_of(XR, r)), tiles(x_of(XO, r)), "x_inner")
            if w.pre is not None:
                o = w.pre.o
                if due(o):
                    pool.wait_ge(sem("hn_mm"), o)
                normalize("proj", o, 2 * o + 2, hn[:, :, :], tiles(x_of(XR, w.pre.b)), "hn")
            if w.post is not None:
                a = w.post
                if due(a.o):
                    pool.wait_ge(sem("hn2_mm"), a.o)
                normalize("post", a.o, 2 * a.o + 2, hn2[:, :, :], tiles(x_of(XR, a.b)), "hn2")
                pool.tensor_tensor(tiles(x_of(XR, a.b)), tiles(x_of(XR, a.b)), b2_row[a.l][:, :, :], ALU.add).then_inc(sem("b2_add"), 1)

        run_steps(pool, step)
        pool_tail(pool)

    @block.vector
    def _(dve):
        def stats(key, buf, b):
            hold(dve, b)
            for t in range(2):
                src = buf[:, t, :] if b is None else tile_of(buf, b, t)
                dve.bn_stats(bn[key][:, t, :], src).then_inc(sem(f"bn_{key}"), 1)

        def aggregate(key, o):
            dve.wait_ge(sem(f"bn_{key}"), 2 * o + 2)
            hold(dve, o)
            for t in range(2):
                dve.bn_aggr(mv[key][:, t, :], bn[key][:, t, :]).then_inc(sem(f"mv_{key}"), 1)

        dve.memset(scratch[:, :], 0.0).then_inc(sem("scratch"), 1)
        dve.memset(nm_parts[:, :, :, :], 0.0).then_inc(sem("scratch"), 1)
        dve.memset(onesb[:, :], 1.0).then_inc(sem("dve_const"), 1)
        dve.wait_ge(sem("scratch"), 2)
        dve.wait_ge(sem("x_first"), 16)
        stats("raw", XO, 0)
        aggregate("raw", 0)
        dve.wait_ge(sem("x_inner"), 1)
        stats("proj", XR, 0)
        aggregate("proj", 0)
        dve.wait_ge(sem("setup_in"), 16 * N_LOADS)
        dve.tensor_copy(identb[:, :], ident[:, :]).then_inc(sem("dve_const"), 1)
        dve.tensor_copy(trib[:, :], consts["tri"][:, :]).then_inc(sem("dve_const"), 1)
        for l in range(L):
            for n, w in ((0, wq), (1, wk)):
                dve.tensor_copy(w[l][:, :].rearrange("p (d h) -> p d h", h=H),
                                w_in[:, 4 * l + n, :].rearrange("p (h d) -> p d h", h=H)).then_inc(sem("w_order"), 1)
            for s in range(2):
                half = slice(64 * s, 64 * s + 64)
                dve.tensor_copy(wv[l][:, half].rearrange("p (g u d) -> p g u d", g=4, u=2),
                                w_in[:, 4 * l + 2, half].rearrange("p (u g d) -> p g u d", g=4, u=2)).then_inc(sem("w_order"), 1)
        for l in range(L):
            dve.tensor_copy(yraw[:, l * P:(l + 1) * P], cols[:, 6, l:l + 1].to_broadcast([P, P])).then_inc(sem("bv_wide"), 1)
        for l in range(L):
            dve.wait_ge(sem("bo_mm"), L)
            dve.tensor_tensor(bo_row[l][:, :, :], bo_row[l][:, :, :], ma_ps[:, l * P:(l + 1) * P].rearrange(
                "p (o c) -> p o c", o=1).to_broadcast([P, 2, P]), ALU.add).then_inc(sem("setup_bo"), 1)

        for l in range(L):
            dve.wait_ge(sem("wo_order_mm"), L)
            dve.tensor_copy(wo[l][:, :], mb_ps[:, l * P:(l + 1) * P]).then_inc(sem("w_order"), 1)
        def minus_max(item, g):
            c = 2 * item.o + g
            m = maxes[item.p][:, 8 * g:8 * g + 8, :].rearrange("p h t -> p (h t)")
            dve.wait_ge(sem("maxed"), 16 * item.o + 8 * g + 8)
            if due(c - 1):
                dve.wait_ge(sem("nm_mm"), c - 1)
            n = nm_parts[:, g]
            dve.tensor_scalar(n[:, 0, :], m, -1.0, None, ALU.mult).then_inc(sem("nm0"), 1)
            dve.wait_ge(sem("nm0"), c + 1)
            dve.scalar_tensor_tensor(out=nm_rest[:, 0, :], in0=m, scalar=-1.0, in1=n[:, 0, :],
                                     op0=ALU.mult, op1=ALU.subtract).then_inc(sem("nm1"), 1)
            dve.wait_ge(sem("nm1"), c + 1)
            dve.tensor_copy(n[:, 1, :], nm_rest[:, 0, :]).then_inc(sem("nm2"), 1)
            dve.wait_ge(sem("nm2"), c + 1)
            dve.tensor_tensor(n[:, 2, :], nm_rest[:, 0, :], n[:, 1, :], ALU.subtract).then_inc(sem("nm_parts"), 1)

        def minus_max_rows(item, g):
            c = 2 * item.o + g
            dve.wait_ge(sem("nm_mm"), c + 1)
            if due(16 * item.o):
                dve.wait_ge(sem(f"max_in{g}"), 16 * item.o)
            dve.tensor_copy(nm_rows[:, g, :], mt_ps[0:48, g, 0:P]).then_inc(sem("nm_rows"), 1)

        def step(w, _):
            for j in range(H):
                if w.next is not None:
                    o = w.next.o
                    dve.wait_ge(sem("sm_mm"), 16 * o + j + 1)
                    dve.tensor_reduce(maxes[w.next.p][:, j, :], sm_ps[j % 2][:, :, :], AX.X, ALU.max).then_inc(sem("maxed"), 1)
                if j == 0 and w.cur is not None:
                    minus_max(w.cur, 1)
                if j == 1 and w.router is not None:
                    f = w.router.b
                    dve.wait_ge(sem("x_attn"), f + 1)
                    if due(f):
                        dve.wait_ge(sem("sub_f3"), f)
                    stats("f3", XO, f)
                    aggregate("f3", f)
                if j == 1 and w.final is not None:
                    f = w.final.b
                    dve.wait_ge(sem("ffn_out"), w.final.o + 1)
                    if due(f):
                        dve.wait_ge(sem("sub_f1"), f)
                    stats("f1", XR, f)
                    aggregate("f1", f)
                if j == 3 and w.cur is not None:
                    minus_max_rows(w.cur, 1)
                if j == 2 and w.raw is not None and not (isinstance(w.raw.b, int) and w.raw.b == 0):
                    r = w.raw.b
                    if isinstance(r, int) and r in (1, 4):
                        dve.wait_ge(sem("x_rest"), 16 if r == 1 else 32)
                    if due(r):
                        dve.wait_ge(sem("sub_raw"), r)
                    stats("raw", XO, r)
                    aggregate("raw", r)
                if j == 4 and w.post is not None:
                    a = w.post
                    dve.wait_ge(sem("yt_mm"), a.o + 1)
                    src = ma_ps[:, :].rearrange("p (n r) -> p n r", r=32)
                    dve.reciprocal(rden[:, :].rearrange("p (n u) -> p n u", u=2), src[:, :, 16:18]).then_inc(sem("rden"), 1)
                    dve.wait_ge(sem("rden"), a.o + 1)
                    if due(a.o):
                        dve.wait_ge(sem("ynt_mm"), a.o)
                    dve.tensor_tensor(yn[:, :, :].rearrange("p (n u) d -> p n u d", u=2),
                                      src[:, :, 0:16].rearrange("p n (u d) -> p n u d", u=2),
                                      rden[:, :].rearrange("p (n u o) -> p n u o", u=2, o=1).to_broadcast([P, H, 2, HD]),
                                      ALU.mult).then_inc(sem("yn"), 1)
                if j == 7 and w.proj is not None:
                    dve.wait_ge(sem("rest"), w.proj.o + 1)
                    dve.tensor_copy(parts[:, 1, :], rest[:, :]).then_inc(sem("part1"), 1)
                if j == 8 and w.next is not None:
                    minus_max(w.next, 0)
                if j == 8 and w.final is not None:
                    f = w.final.b
                    dve.wait_ge(sem("f1_b"), f + 1)
                    if due(f):
                        dve.wait_ge(sem("sub_f2"), f)
                    stats("f2", fin, None)
                    aggregate("f2", f)
                if j == 10 and w.next is not None:
                    minus_max_rows(w.next, 0)
            if w.last is not None:
                e = w.last
                dve.wait_ge(sem("w2_mm"), e.o + 1)
                dve.wait_ge(sem("b2_add"), e.o + 1)
                dve.tensor_tensor(x_of(XR, e.b), ma_ps[:, 0:2 * P], x_of(XR, e.b), ALU.add).then_inc(sem("ffn_out"), 1)
            if w.pre is not None:
                if w.pre.l == 0:
                    dve.wait_ge(sem("x_inner"), w.pre.b + 1)
                elif w.last is not None:
                    dve.wait_ge(sem("ffn_out"), w.last.o + 1)
                if due(w.pre.o):
                    dve.wait_ge(sem("sub_proj"), w.pre.o)
                stats("proj", XR, w.pre.b)
                aggregate("proj", w.pre.o)
            if w.post is not None:
                a = w.post
                dve.wait_ge(sem("wo_mm"), a.o + 1)
                dve.wait_ge(sem("bo_add"), a.o + 1)
                dve.tensor_tensor(x_of(XR, a.b), ma_ps[:, 0:2 * P], x_of(XR, a.b), ALU.add).then_inc(sem("attn_out"), 1)
                dve.wait_ge(sem("attn_out"), a.o + 1)
                if due(a.o):
                    dve.wait_ge(sem("sub_post"), a.o)
                stats("post", XR, a.b)
                aggregate("post", a.o)

        for p in range(2):
            for h in range(0, H, 4):
                last = dve.tensor_copy(qst[p][0:ROWS, h:h + 4, :],
                                       consts["qrows"][0:ROWS, :].rearrange("p (o t) -> p o t", o=1).to_broadcast([ROWS, 4, T]))
        last.then_inc(sem("stack_const"), 1)

        run_steps(dve, step, -2)
        vector_tail(dve)

    @block.scalar
    def _(act):
        def step(w, _):
            for j in range(H):
                if w.cur is not None:
                    k = w.cur
                    act.wait_ge(sem("st_mm"), 16 * k.o + j + 1)
                    if due(4 * k.o + j // 4 - 1):
                        act.wait_ge(sem("pv_mm"), 4 * k.o + j // 4 - 1)
                    act.activation(probs[:, j % 8, :], st_ps[j % 2][:, :, :].rearrange("p a b -> p (a b)"),
                                   ACT.Exp, scale=SCALE).then_inc(sem("exp"), 1)
                if j == 1 and w.post is not None:
                    a = w.post
                    act.wait_ge(sem("pv_mm"), 4 * a.o + 4)
                    if due(a.o):
                        act.wait_ge(sem("yt_mm"), a.o)
                    act.activation(yraw[:, :], pv_ps[:, :], ACT.Copy).then_inc(sem("yraw"), 1)
                if j == 1 and w.next is not None:
                    c = w.next
                    act.wait_ge(sem("v_mm"), c.o + 1)
                    if due(4 * (c.o - 1)):
                        act.wait_ge(sem("pv_mm"), 4 * (c.o - 1))
                    act.wait_ge(sem("v_ones"), 4)
                    for u in range(2):
                        dst = vpad[c.p][:, :, :, :].rearrange("p t (n u) c -> p t n u c", u=2)[:, :, :, u, 8 * u:8 * u + HD]
                        src = ma_ps[:, 0:2 * P].rearrange("p (t n u d) -> p t n u d", t=2, u=2, d=HD)[:, :, :, u, :]
                        last = act.activation(dst, src, ACT.Copy)
                    last.then_inc(sem("v_in"), 1)
                if j == 2 and w.proj is not None:
                    c = w.proj
                    act.wait_ge(sem("hn_mm"), c.o + 1)
                    if due(c.o):
                        act.wait_ge(sem("v_mm"), c.o)
                    act.activation(hT[:, :], mb_ps[:, 0:T], ACT.Identity, scale=cols[:, 0, c.l:c.l + 1],
                                   bias=cols[:, 1, c.l:c.l + 1]).then_inc(sem("hT"), 1)
                if j == 4 and w.proj is not None:
                    c = w.proj
                    act.wait_ge(sem("qk_mm"), c.o + 1)
                    if due(c.o):
                        act.wait_ge(sem("rest"), c.o)
                    if due(16 * c.o):
                        act.wait_ge(sem("parts_out"), 16 * c.o)
                    for side in range(2):
                        half = slice(side * T, (side + 1) * T)
                        bias = cols[:, 2 + side, c.l:c.l + 1]
                        act.activation(qk32[:, half], mb_ps[:, half], ACT.Identity, bias=bias)
                        last = act.activation(parts[:, 0, half], mb_ps[:, half], ACT.Identity, bias=bias)
                    last.then_inc(sem("qk32"), 1)
                if j == 6 and w.last is not None:
                    a = w.last
                    act.wait_ge(sem("hn2_mm"), a.o + 1)
                    if due(2 * a.o):
                        act.wait_ge(sem("u_mm"), 2 * a.o)
                    act.activation(h2T[:, :], mb_ps[:, 0:T], ACT.Identity, scale=cols[:, 4, a.l:a.l + 1],
                                   bias=cols[:, 5, a.l:a.l + 1]).then_inc(sem("h2T"), 1)
                if j == 8 and w.last is not None:
                    a = w.last
                    if due(a.o):
                        act.wait_ge(sem("w2_mm"), a.o)
                    for c in range(NCH):
                        act.wait_ge(sem("u_mm"), 2 * a.o + 1 + c // 2)
                        src = (ma_ps, mb_ps)[c // 2]
                        act.activation(gel[:, c, :], src[:, (c % 2) * T:(c % 2 + 1) * T], ACT.Gelu,
                                       bias=cols[:, 7 + c, a.l:a.l + 1]).then_inc(sem("gelu"), 1)
                if j == 13 and w.post is not None:
                    a = w.post
                    act.wait_ge(sem("ynt_mm"), a.o + 1)
                    if due(a.o):
                        act.wait_ge(sem("wo_mm"), a.o)
                    act.activation(yT[:, :], mb_ps[:, 0:T], ACT.Copy).then_inc(sem("yT"), 1)

        act.wait_ge(sem("setup_in"), 16 * N_LOADS)
        for p in range(2):
            for h in range(0, H, 4):
                last = act.activation(kst[p][0:ROWS, h:h + 4, :], consts["krows"][0:ROWS, :].rearrange(
                    "p (o t) -> p o t", o=1).to_broadcast([ROWS, 4, T]), ACT.Copy)
        last.then_inc(sem("stack_const"), 1)
        run_steps(act, step)
        scalar_tail(act)

    @block.tensor
    def _(pe):
        pe.wait_ge(sem("setup_in"), 16 * N_LOADS)
        pe.wait_ge(sem("dve_const"), 3)
        pe.wait_ge(sem("bv_wide"), L)
        for l in range(L):
            pe.matmul(ma_ps[:, l * P:(l + 1) * P], yraw[:, l * P:(l + 1) * P], w_in[:, 4 * l + 3, :],
                      start=True, stop=True).then_inc(sem("bo_mm"), 1)
            pe.matmul(mb_ps[:, l * P:(l + 1) * P], consts["perm"][:, :], w_in[:, 4 * l + 3, :],
                      start=True, stop=True).then_inc(sem("wo_order_mm"), 1)
        pe.wait_ge(sem("setup_bo"), L)
        pe.wait_ge(sem("w_order"), 5 * L)

        def scores(bank, item, h, maxima, masked, transposed):
            rows = slice(0 if masked else ROW_PROD, ROWS if maxima else ROW_MAX)
            for a in range(2):
                b = a if masked else 1 - a
                x, y = (kst, qst) if transposed else (qst, kst)
                last = pe.matmul(bank[:, a, b * P:(b + 1) * P], x[item.p][rows, h, a * P:(a + 1) * P],
                                 y[item.p][rows, h, b * P:(b + 1) * P], start=True, stop=True)
            return last

        def weigh(item, q):
            pe.wait_ge(sem("exp"), 16 * item.o + 4 * q + 4)
            if q == 0:
                if due(item.o):
                    pe.wait_ge(sem("yraw"), item.o)
            s, u = q // 2, q % 2
            for t in range(2):
                for g in range(4):
                    h = 8 * s + 4 * u + g
                    last = pe.matmul(pv_ps[32 * g:32 * g + 32, s * T:(s + 1) * T],
                                     vpad[item.p][:, t, 8 * s + 2 * g + u, :],
                                     probs[:, h % 8, t * T:(t + 1) * T],
                                     start=(u == 0 and t == 0), stop=(u == 1 and t == 1),
                                     tile_position=(0, 32 * g), skip_group_check=True)
            last.then_inc(sem("pv_mm"), 1)

        def turn_maxima(item, g):
            c = 2 * item.o + g
            pe.wait_ge(sem("nm_parts"), c + 1)
            if due(c):
                pe.wait_ge(sem("nm_rows"), c)
            pe.transpose(mt_ps[:, g, 0:P], nm_parts[:, g, :, :].rearrange("p a b -> p (a b)"),
                         identb[:, :]).then_inc(sem("nm_mm"), 1)

        def row_scores(k, h):
            if h % 8 == 0:
                if due(96 * (k.o + 1)):
                    pe.wait_ge(sem(f"stack_in{h // 8}"), 96 * (k.o + 1))
            if due(16 * k.o + h - 1):
                pe.wait_ge(sem("maxed"), 16 * k.o + h - 1)
            scores(sm_ps[h % 2], k, h, False, True, False)
            scores(sm_ps[h % 2], k, h, False, False, False).then_inc(sem("sm_mm"), 1)

        def step(w, _):
            for j in range(H):
                if w.cur is not None:
                    k = w.cur
                    if j % 8 == 0:
                        if due(96 * (k.o + 1)):
                            pe.wait_ge(sem(f"stack_in{j // 8}"), 96 * (k.o + 1))
                        if due(16 * (k.o + 1)):
                            pe.wait_ge(sem(f"max_in{j // 8}"), 16 * (k.o + 1))
                    if j == 0:
                        pe.wait_ge(sem("v_in"), k.o + 1)
                    if due(16 * k.o + j - 1):
                        pe.wait_ge(sem("exp"), 16 * k.o + j - 1)
                    scores(st_ps[j % 2], k, j, True, True, True)
                if w.next is not None and j <= 10:
                    row_scores(w.next, j)
                if w.cur is not None:
                    scores(st_ps[j % 2], w.cur, j, True, False, True).then_inc(sem("st_mm"), 1)
                if w.next is not None and j in (10, 11, 12):
                    for h in {10: (11, 12, 13), 11: (14,), 12: (15,)}[j]:
                        row_scores(w.next, h)
                if j == 1 and w.post is not None:
                    weigh(w.post, 3)
                if j == 1 and w.next is not None:
                    c = w.next
                    if w.last is not None:
                        pe.wait_ge(sem("attn_out"), w.last.o + 1)
                    else:
                        if due(c.o):
                            pe.wait_ge(sem("v_in"), c.o)
                        if w.old is not None:
                            pe.wait_ge(sem("ffn_out"), w.old.o + 1)
                    for t in range(2):
                        last = pe.matmul(ma_ps[:, t * P:(t + 1) * P], hT[:, t * P:(t + 1) * P], wv[c.l][:, :],
                                         start=True, stop=True)
                    last.then_inc(sem("v_mm"), 1)
                if j == 2 and w.cur is not None:
                    turn_maxima(w.cur, 1)
                if j == 2 and w.proj is not None:
                    c = w.proj
                    if due(c.o):
                        pe.wait_ge(sem("qk32"), c.o)
                    pe.wait_ge(sem("hn"), c.o + 1)
                    for t in range(2):
                        last = pe.transpose(mb_ps[:, t * P:(t + 1) * P], hn[:, t, :], ident[:, :])
                    last.then_inc(sem("hn_mm"), 1)
                if j == 3 and w.post is not None:
                    a = w.post
                    if w.next is not None:
                        pe.wait_ge(sem("v_in"), w.next.o + 1)
                    elif w.last is not None:
                        pe.wait_ge(sem("attn_out"), w.last.o + 1)
                    elif w.old is not None:
                        pe.wait_ge(sem("ffn_out"), w.old.o + 1)
                    pe.wait_ge(sem("yraw"), a.o + 1)
                    for n in range(4):
                        m = 2 * (n % 2) + n // 2
                        last = pe.transpose(ma_ps[:, m * P:(m + 1) * P], yraw[:, n * P:(n + 1) * P], ident[:, :])
                    last.then_inc(sem("yt_mm"), 1)
                if j == 4 and w.proj is not None:
                    c = w.proj
                    pe.wait_ge(sem("hT"), c.o + 1)
                    for side, wt in enumerate((wq, wk)):
                        last = pe.matmul(mb_ps[:, side * T:(side + 1) * T], wt[c.l][:, :], hT[:, :], start=True, stop=True)
                    last.then_inc(sem("qk_mm"), 1)
                if j == 5 and w.cur is not None:
                    weigh(w.cur, 0)
                if j == 6 and w.last is not None:
                    a = w.last
                    if w.proj is not None:
                        pe.wait_ge(sem("qk32"), w.proj.o + 1)
                    pe.wait_ge(sem("hn2"), a.o + 1)
                    for t in range(2):
                        last = pe.transpose(mb_ps[:, t * P:(t + 1) * P], hn2[:, t, :], ident[:, :])
                    last.then_inc(sem("hn2_mm"), 1)
                if j == 8 and w.last is not None:
                    a = w.last
                    if w.post is not None:
                        pe.wait_ge(sem("yn"), w.post.o + 1)
                    elif w.next is not None:
                        pe.wait_ge(sem("v_in"), w.next.o + 1)
                    else:
                        pe.wait_ge(sem("attn_out"), a.o + 1)
                    pe.wait_ge(sem("h2T"), a.o + 1)
                    for m, bank in enumerate((ma_ps, mb_ps)):
                        for c in range(2):
                            last = pe.matmul(bank[:, c * T:(c + 1) * T], w1[a.l][:, (2 * m + c) * P:(2 * m + c + 1) * P],
                                             h2T[:, :], start=True, stop=True)
                        last.then_inc(sem("u_mm"), 1)
                if j == 9 and w.cur is not None:
                    weigh(w.cur, 1)
                if j == 9 and w.next is not None:
                    turn_maxima(w.next, 0)
                if j == 12 and w.last is not None:
                    e = w.last
                    pe.wait_ge(sem("gelu"), 4 * e.o + 4)
                    for t in range(2):
                        for c in range(NCH):
                            last = pe.matmul(ma_ps[:, t * P:(t + 1) * P], gel[:, c, t * P:(t + 1) * P],
                                             w2[e.l][:, c, :], start=(c == 0), stop=(c == NCH - 1))
                    last.then_inc(sem("w2_mm"), 1)
                if j == 13 and w.cur is not None:
                    weigh(w.cur, 2)
                if j == 13 and w.post is not None:
                    a = w.post
                    if w.last is None:
                        if w.proj is not None:
                            pe.wait_ge(sem("qk32"), w.proj.o + 1)
                        elif w.next is not None:
                            pe.wait_ge(sem("qk32"), w.next.o + 1)
                    pe.wait_ge(sem("yn"), a.o + 1)
                    yv = yn[:, :, :].rearrange("p (t m) d -> p t (m d)", t=2)
                    for t in range(2):
                        last = pe.transpose(mb_ps[:, t * P:(t + 1) * P], yv[:, t, :], ident[:, :])
                    last.then_inc(sem("ynt_mm"), 1)
                if j == 15 and w.post is not None:
                    a = w.post
                    if w.last is not None:
                        pe.wait_ge(sem("ffn_out"), w.last.o + 1)
                    pe.wait_ge(sem("yT"), a.o + 1)
                    for t in range(2):
                        last = pe.matmul(ma_ps[:, t * P:(t + 1) * P], yT[:, t * P:(t + 1) * P], wo[a.l][:, :],
                                         start=True, stop=True)
                    last.then_inc(sem("wo_mm"), 1)

        run_steps(pe, step)
        tensor_tail(pe)


_INS = ["L0_attn_" + n for n in ("x", "ln1_g", "ln1_b", "wq", "bq", "wk", "bk", "wv", "bv", "wo", "bo", "ln2_g", "ln2_b",
                                 "w1", "b1", "w2", "b2", "lnf_g", "lnf_b")]
_INS += ["L0_ffn_w_" + n for n in ("router", "gate", "up", "down")]


def kernel(**inputs):
    import concourse.bacc as _bacc
    from concourse.bass_utils import run_bass_kernel_spmd as _run

    nc = _bacc.Bacc("TRN2", target_bir_lowering=False, num_devices=1)
    arrays, aps = {}, {}
    given = {name: np.ascontiguousarray(inputs[name]) for name in _INS}
    given.update({"const_" + k: v for k, v in constants().items()})
    for name, a in given.items():
        arrays[f"in_{name}"] = a
        aps[name] = nc.dram_tensor(f"in_{name}", a.shape, mybir.dt.from_np(a.dtype), kind="ExternalInput").ap()
    out = nc.dram_tensor("out_0", (NB, T, P), F32, kind="ExternalOutput").ap()
    build(nc, aps, out)
    r = _run(nc, [arrays], core_ids=[0])
    return r.results[0]["out_0"]
```
